# Optimizing a Trainium2 kernel written in Bass

```python
import numpy as np
import jax
import jax.numpy as jnp

def _softmax(x, axis=-1):
    return jax.nn.softmax(x, axis=axis)
def _gelu(x):
    return jax.nn.gelu(x, approximate=True)
def _silu(x):
    return jax.nn.silu(x)
def _sigmoid(x):
    return jax.nn.sigmoid(x)
def _layernorm(x, axis=-1, eps=1e-5):
    m = jnp.mean(x, axis=axis, keepdims=True)
    v = jnp.var(x, axis=axis, keepdims=True)
    return (x - m) / jnp.sqrt(v + eps)
def _scatter_add(tgt, idx, src, axis=0):
    return tgt.at[idx].add(src)
def _segment_sum(src, seg, n):
    return jax.ops.segment_sum(src, seg, n)

kernel_name = 'mk_conv_preact_d2_conv_nchw96_7a4a91'

def setup_inputs(seed: int = 0):
    np.random.seed(seed)
    _w = jnp.asarray
    def _rec_inputs():
        import jax
        import jax.numpy as jnp
        _gk = jax.random.key(seed)
        x = -0.0004039 + 1 * jax.random.normal(jax.random.fold_in(_gk, 1), (2, 96, 256, 256), jnp.float32)
        return x
    x = _rec_inputs()
    def _L0_conv_setup():
        import jax, jax.numpy as jnp
        import numpy as np
        from functools import partial
        EPS = 1e-05

        def _positions(size, step, ps):
            pos = []
            for i in range(0, size + step - ps, step):
                t = i
                if i + ps > size:
                    t = size - ps
                pos.append(t)
            return np.asarray(pos, dtype=np.int32)

        def _div_factor(size, step, ps):
            f = np.ones(size, dtype=np.float32)
            for i in range(step, size + step - ps, step):
                top, down = (i, i + ps - step)
                if top + ps > size:
                    top = size - ps
                f[top:down] *= 0.5
            return f

        def _layernorm(x, w, b):
            m = jnp.mean(x, axis=-1, keepdims=True)
            v = jnp.var(x, axis=-1, keepdims=True)
            return (x - m) / jnp.sqrt(v + EPS) * w + b

        def _gelu(x):
            return jax.nn.gelu(x, approximate=False)
        HEADS = 4
        key = jax.random.key(seed)
        ks = jax.random.split(key, 8)
        dim, qk_dim, mlp_dim = (96, 64, 192)
        b, h, w = (2, 256, 256)
        s = lambda fan: 1.0 / np.sqrt(fan)
        return {'x': jax.random.normal(ks[0], (b, dim, h, w), jnp.float32), 'norm1_w': jnp.ones((dim,), jnp.float32), 'norm1_b': jnp.zeros((dim,), jnp.float32), 'wq': jax.random.normal(ks[1], (dim, qk_dim), jnp.float32) * s(dim), 'wk': jax.random.normal(ks[2], (dim, qk_dim), jnp.float32) * s(dim), 'wv': jax.random.normal(ks[3], (dim, dim), jnp.float32) * s(dim), 'wproj': jax.random.normal(ks[4], (dim, dim), jnp.float32) * s(dim), 'norm2_w': jnp.ones((dim,), jnp.float32), 'norm2_b': jnp.zeros((dim,), jnp.float32), 'fc1_w': jax.random.normal(ks[5], (dim, mlp_dim), jnp.float32) * s(dim), 'fc1_b': jnp.zeros((mlp_dim,), jnp.float32), 'dw_w': jax.random.normal(ks[6], (mlp_dim, 1, 5, 5), jnp.float32) * s(25), 'dw_b': jnp.zeros((mlp_dim,), jnp.float32), 'fc2_w': jax.random.normal(ks[7], (mlp_dim, dim), jnp.float32) * s(mlp_dim), 'fc2_b': jnp.zeros((dim,), jnp.float32), 'ps': 16}
    _L0_conv_all = _L0_conv_setup()
    _L0_conv_in = {k: v for k, v in _L0_conv_all.items() if k in ('norm1_w', 'norm1_b', 'wq', 'wk', 'wv', 'wproj', 'norm2_w', 'norm2_b', 'fc1_w', 'fc1_b', 'dw_w', 'dw_b', 'fc2_w', 'fc2_b', )}
    del _L0_conv_all

    def _L1_conv_setup():
        import jax, jax.numpy as jnp
        import numpy as np
        HEADS, HEAD_DIM = (4, 24)
        FOLD = 2
        PROP = 2
        EPS = 1e-12

        def _conv1x1(x, w, b):
            return jnp.einsum('bchw,oc->bohw', x, w) + b[None, :, None, None]

        def _l2norm(x):
            n = jnp.sqrt(jnp.sum(x * x, axis=-1, keepdims=True))
            return x / jnp.maximum(n, EPS)

        def _cluster_fwd(x, f_w, f_b, v_w, v_b, proj_w, proj_b, sim_alpha, sim_beta):
            B, dim, W0, H0 = x.shape
            e, c = (HEADS, HEAD_DIM)
            value = _conv1x1(x, v_w, v_b)
            feat = _conv1x1(x, f_w, f_b)

            def split_heads(t):
                return t.reshape(B, e, c, W0, H0).reshape(B * e, c, W0, H0)
            feat, value = (split_heads(feat), split_heads(value))
            w, h = (W0 // FOLD, H0 // FOLD)

            def fold(t):
                b0 = t.shape[0]
                t = t.reshape(b0, c, FOLD, w, FOLD, h).transpose(0, 2, 4, 1, 3, 5)
                return t.reshape(b0 * FOLD * FOLD, c, w, h)
            feat, value = (fold(feat), fold(value))
            b = feat.shape[0]
            N, M = (w * h, PROP * PROP)

            def pool(t):
                return t.reshape(b, c, PROP, w // PROP, PROP, h // PROP).mean(axis=(3, 5))
            centers = pool(feat)
            value_centers = pool(value).reshape(b, c, M).transpose(0, 2, 1)
            pts = feat.reshape(b, c, N).transpose(0, 2, 1)
            ctr = centers.reshape(b, c, M).transpose(0, 2, 1)
            sim = jax.nn.sigmoid(sim_beta + sim_alpha * jnp.einsum('bmc,bnc->bmn', _l2norm(ctr), _l2norm(pts)))
            idx = jnp.argmax(sim, axis=1)
            mask = (jnp.arange(M)[None, :, None] == idx[:, None, :]).astype(sim.dtype)
            sim = sim * mask
            value2 = value.reshape(b, c, N).transpose(0, 2, 1)
            agg = (jnp.einsum('bmn,bnc->bmc', sim, value2) + value_centers) / (jnp.sum(sim, axis=-1, keepdims=True) + 1.0)
            out = jnp.einsum('bmc,bmn->bnc', agg, sim)
            out = out.transpose(0, 2, 1).reshape(b, c, w, h)
            b0 = b // (FOLD * FOLD)
            out = out.reshape(b0, FOLD, FOLD, c, w, h).transpose(0, 3, 1, 4, 2, 5)
            out = out.reshape(b0, c, W0, H0)
            out = out.reshape(B, e * c, W0, H0)
            return _conv1x1(out, proj_w, proj_b)
        key = jax.random.key(seed)
        ks = jax.random.split(key, 8)
        dim = HEADS * HEAD_DIM
        B, H, W = (8, 128, 128)
        return {'x': jax.random.normal(ks[0], (B, dim, H, W), jnp.float32), 'f_w': jax.random.normal(ks[1], (dim, dim), jnp.float32) * 0.05, 'f_b': jnp.zeros((dim,), jnp.float32), 'v_w': jax.random.normal(ks[2], (dim, dim), jnp.float32) * 0.05, 'v_b': jnp.zeros((dim,), jnp.float32), 'proj_w': jax.random.normal(ks[3], (dim, dim), jnp.float32) * 0.05, 'proj_b': jnp.zeros((dim,), jnp.float32), 'sim_alpha': jnp.ones((1,), jnp.float32), 'sim_beta': jnp.zeros((1,), jnp.float32)}
    _L1_conv_all = _L1_conv_setup()
    _L1_conv_in = {k: v for k, v in _L1_conv_all.items() if k in ('f_w', 'f_b', 'v_w', 'v_b', 'proj_w', 'proj_b', 'sim_alpha', 'sim_beta', )}
    del _L1_conv_all

    return {
        "x": x,
        "L0_conv_norm1_w": _L0_conv_in["norm1_w"],
        "L0_conv_norm1_b": _L0_conv_in["norm1_b"],
        "L0_conv_wq": _L0_conv_in["wq"],
        "L0_conv_wk": _L0_conv_in["wk"],
        "L0_conv_wv": _L0_conv_in["wv"],
        "L0_conv_wproj": _L0_conv_in["wproj"],
        "L0_conv_norm2_w": _L0_conv_in["norm2_w"],
        "L0_conv_norm2_b": _L0_conv_in["norm2_b"],
        "L0_conv_fc1_w": _L0_conv_in["fc1_w"],
        "L0_conv_fc1_b": _L0_conv_in["fc1_b"],
        "L0_conv_dw_w": _L0_conv_in["dw_w"],
        "L0_conv_dw_b": _L0_conv_in["dw_b"],
        "L0_conv_fc2_w": _L0_conv_in["fc2_w"],
        "L0_conv_fc2_b": _L0_conv_in["fc2_b"],
        "L1_conv_f_w": _L1_conv_in["f_w"],
        "L1_conv_f_b": _L1_conv_in["f_b"],
        "L1_conv_v_w": _L1_conv_in["v_w"],
        "L1_conv_v_b": _L1_conv_in["v_b"],
        "L1_conv_proj_w": _L1_conv_in["proj_w"],
        "L1_conv_proj_b": _L1_conv_in["proj_b"],
        "L1_conv_sim_alpha": _L1_conv_in["sim_alpha"],
        "L1_conv_sim_beta": _L1_conv_in["sim_beta"],
    }

def reference(x, L0_conv_norm1_w, L0_conv_norm1_b, L0_conv_wq, L0_conv_wk, L0_conv_wv, L0_conv_wproj, L0_conv_norm2_w, L0_conv_norm2_b, L0_conv_fc1_w, L0_conv_fc1_b, L0_conv_dw_w, L0_conv_dw_b, L0_conv_fc2_w, L0_conv_fc2_b, L1_conv_f_w, L1_conv_f_b, L1_conv_v_w, L1_conv_v_b, L1_conv_proj_w, L1_conv_proj_b, L1_conv_sim_alpha, L1_conv_sim_beta):
    import jax
    import jax.numpy as jnp
    def _L0_conv_ref(x, norm1_w, norm1_b, wq, wk, wv, wproj, norm2_w, norm2_b, fc1_w, fc1_b, dw_w, dw_b, fc2_w, fc2_b, ps):
        import jax, jax.numpy as jnp
        import numpy as np
        from functools import partial
        EPS = 1e-05

        def _positions(size, step, ps):
            pos = []
            for i in range(0, size + step - ps, step):
                t = i
                if i + ps > size:
                    t = size - ps
                pos.append(t)
            return np.asarray(pos, dtype=np.int32)

        def _div_factor(size, step, ps):
            f = np.ones(size, dtype=np.float32)
            for i in range(step, size + step - ps, step):
                top, down = (i, i + ps - step)
                if top + ps > size:
                    top = size - ps
                f[top:down] *= 0.5
            return f

        def _layernorm(x, w, b):
            m = jnp.mean(x, axis=-1, keepdims=True)
            v = jnp.var(x, axis=-1, keepdims=True)
            return (x - m) / jnp.sqrt(v + EPS) * w + b

        def _gelu(x):
            return jax.nn.gelu(x, approximate=False)
        HEADS = 4
        b, c, h, w = x.shape
        step = ps - 2
        if h == ps and w == ps:
            step = ps
        tops = _positions(h, step, ps)
        lefts = _positions(w, step, ps)
        nh, nw = (len(tops), len(lefts))
        n = nh * nw
        row_idx = tops[:, None] + np.arange(ps)
        col_idx = lefts[:, None] + np.arange(ps)
        crop = x[:, :, row_idx[:, None, :, None], col_idx[None, :, None, :]]
        tok = crop.transpose(0, 2, 3, 4, 5, 1).reshape(b * n, ps * ps, c)
        y = _layernorm(tok, norm1_w, norm1_b)
        qk_dim = wq.shape[1]
        hd_q = qk_dim // HEADS
        hd_v = c // HEADS
        q = (y @ wq).reshape(b * n, ps * ps, HEADS, hd_q).transpose(0, 2, 1, 3)
        k = (y @ wk).reshape(b * n, ps * ps, HEADS, hd_q).transpose(0, 2, 1, 3)
        v = (y @ wv).reshape(b * n, ps * ps, HEADS, hd_v).transpose(0, 2, 1, 3)
        scores = jnp.einsum('bhnd,bhmd->bhnm', q, k) / jnp.sqrt(jnp.float32(hd_q))
        attn = jax.nn.softmax(scores, axis=-1)
        out = jnp.einsum('bhnm,bhmd->bhnd', attn, v)
        out = out.transpose(0, 2, 1, 3).reshape(b * n, ps * ps, c)
        tok = out @ wproj + tok
        crop = tok.reshape(b, nh, nw, ps, ps, c).transpose(0, 5, 1, 2, 3, 4)
        acc = jnp.zeros_like(x)
        acc = acc.at[:, :, row_idx[:, None, :, None], col_idx[None, :, None, :]].add(crop)
        fh = jnp.asarray(_div_factor(h, step, ps))
        fw = jnp.asarray(_div_factor(w, step, ps))
        x2 = acc * fh[None, None, :, None] * fw[None, None, None, :]
        tok2 = x2.transpose(0, 2, 3, 1).reshape(b, h * w, c)
        y = _layernorm(tok2, norm2_w, norm2_b)
        y = _gelu(y @ fc1_w + fc1_b)
        mlp = y.shape[-1]
        ymap = y.transpose(0, 2, 1).reshape(b, mlp, h, w)
        dw = jax.lax.conv_general_dilated(ymap, dw_w, window_strides=(1, 1), padding=((2, 2), (2, 2)), dimension_numbers=('NCHW', 'OIHW', 'NCHW'), feature_group_count=mlp)
        dw = _gelu(dw + dw_b[None, :, None, None])
        y = y + dw.reshape(b, mlp, h * w).transpose(0, 2, 1)
        tok2 = y @ fc2_w + fc2_b + tok2
        return tok2.reshape(b, h, w, c).transpose(0, 3, 1, 2)

    def _L1_conv_ref(x, f_w, f_b, v_w, v_b, proj_w, proj_b, sim_alpha, sim_beta):
        import jax, jax.numpy as jnp
        import numpy as np
        HEADS, HEAD_DIM = (4, 24)
        FOLD = 2
        PROP = 2
        EPS = 1e-12

        def _conv1x1(x, w, b):
            return jnp.einsum('bchw,oc->bohw', x, w) + b[None, :, None, None]

        def _l2norm(x):
            n = jnp.sqrt(jnp.sum(x * x, axis=-1, keepdims=True))
            return x / jnp.maximum(n, EPS)

        def _cluster_fwd(x, f_w, f_b, v_w, v_b, proj_w, proj_b, sim_alpha, sim_beta):
            B, dim, W0, H0 = x.shape
            e, c = (HEADS, HEAD_DIM)
            value = _conv1x1(x, v_w, v_b)
            feat = _conv1x1(x, f_w, f_b)

            def split_heads(t):
                return t.reshape(B, e, c, W0, H0).reshape(B * e, c, W0, H0)
            feat, value = (split_heads(feat), split_heads(value))
            w, h = (W0 // FOLD, H0 // FOLD)

            def fold(t):
                b0 = t.shape[0]
                t = t.reshape(b0, c, FOLD, w, FOLD, h).transpose(0, 2, 4, 1, 3, 5)
                return t.reshape(b0 * FOLD * FOLD, c, w, h)
            feat, value = (fold(feat), fold(value))
            b = feat.shape[0]
            N, M = (w * h, PROP * PROP)

            def pool(t):
                return t.reshape(b, c, PROP, w // PROP, PROP, h // PROP).mean(axis=(3, 5))
            centers = pool(feat)
            value_centers = pool(value).reshape(b, c, M).transpose(0, 2, 1)
            pts = feat.reshape(b, c, N).transpose(0, 2, 1)
            ctr = centers.reshape(b, c, M).transpose(0, 2, 1)
            sim = jax.nn.sigmoid(sim_beta + sim_alpha * jnp.einsum('bmc,bnc->bmn', _l2norm(ctr), _l2norm(pts)))
            idx = jnp.argmax(sim, axis=1)
            mask = (jnp.arange(M)[None, :, None] == idx[:, None, :]).astype(sim.dtype)
            sim = sim * mask
            value2 = value.reshape(b, c, N).transpose(0, 2, 1)
            agg = (jnp.einsum('bmn,bnc->bmc', sim, value2) + value_centers) / (jnp.sum(sim, axis=-1, keepdims=True) + 1.0)
            out = jnp.einsum('bmc,bmn->bnc', agg, sim)
            out = out.transpose(0, 2, 1).reshape(b, c, w, h)
            b0 = b // (FOLD * FOLD)
            out = out.reshape(b0, FOLD, FOLD, c, w, h).transpose(0, 3, 1, 4, 2, 5)
            out = out.reshape(b0, c, W0, H0)
            out = out.reshape(B, e * c, W0, H0)
            return _conv1x1(out, proj_w, proj_b)
        return _cluster_fwd(x, f_w, f_b, v_w, v_b, proj_w, proj_b, sim_alpha, sim_beta)

    def _gn(v, G=32, eps=1e-5):
        B_, C_, H_, W_ = v.shape
        g = v.reshape(B_, G, C_ // G, H_, W_)
        m = jnp.mean(g, axis=(2, 3, 4), keepdims=True)
        s = jnp.var(g, axis=(2, 3, 4), keepdims=True)
        return ((g - m) / jnp.sqrt(s + eps)).reshape(v.shape)

    def _ln_c(v, eps=1e-6):
        m = jnp.mean(v, axis=1, keepdims=True)
        s = jnp.var(v, axis=1, keepdims=True)
        return (v - m) / jnp.sqrt(s + eps)

    def _ln_t(v, eps=1e-5):
        m = jnp.mean(v, axis=-1, keepdims=True)
        s = jnp.var(v, axis=-1, keepdims=True)
        return (v - m) / jnp.sqrt(s + eps)

    def _to_tokens(v):
        B_, C_, H_, W_ = v.shape
        return v.reshape(B_, C_, H_ * W_).transpose(0, 2, 1)
    def _from_tokens(t, like):
        B_, C_, H_, W_ = like.shape
        return t.transpose(0, 2, 1).reshape(B_, C_, H_, W_)

    x = x + _L0_conv_ref(_gn(x), L0_conv_norm1_w, L0_conv_norm1_b, L0_conv_wq, L0_conv_wk, L0_conv_wv, L0_conv_wproj, L0_conv_norm2_w, L0_conv_norm2_b, L0_conv_fc1_w, L0_conv_fc1_b, L0_conv_dw_w, L0_conv_dw_b, L0_conv_fc2_w, L0_conv_fc2_b, 16)
    x = x + _L1_conv_ref(_gn(x), L1_conv_f_w, L1_conv_f_b, L1_conv_v_w, L1_conv_v_b, L1_conv_proj_w, L1_conv_proj_b, L1_conv_sim_alpha, L1_conv_sim_beta)
    return x


_drawn_inputs = setup_inputs


def setup_inputs(seed=0):
    import zlib

    import numpy as np

    out = dict(_drawn_inputs(seed))
    spreads = {'L0_conv_norm1_w': (1.0, 0.2),
     'L0_conv_norm1_b': (0.0, 0.1),
     'L0_conv_norm2_w': (1.0, 0.2),
     'L0_conv_norm2_b': (0.0, 0.1),
     'L0_conv_fc1_b': (0.0, 0.1),
     'L0_conv_dw_b': (0.0, 0.1),
     'L0_conv_fc2_b': (0.0, 0.1),
     'L1_conv_f_b': (0.0, 0.8),
     'L1_conv_v_b': (0.0, 0.516),
     'L1_conv_proj_b': (0.0, 0.1)}
    factors = {'L1_conv_f_w': 7.205, 'L1_conv_v_w': 3.229}
    for name, (base, spread) in spreads.items():
        noise = np.random.default_rng([zlib.crc32(name.encode()), seed]).standard_normal(out[name].shape)
        drawn = base * np.exp(spread * noise) if base else spread * noise
        out[name] = jnp.asarray(drawn.astype(out[name].dtype))
    for name, factor in factors.items():
        out[name] = (out[name] * factor).astype(out[name].dtype)
    return out
```

```python
from contextlib import ExitStack

import numpy as np

import concourse.bass as bass
from concourse import mybir

F32 = mybir.dt.float32
BF16 = mybir.dt.bfloat16
ALU = mybir.AluOpType
ACT = mybir.ActivationFunctionType
AX = mybir.AxisListType

B, C, H, W = 2, 96, 256, 256
PS, STEP = 16, 14
NWIN = 19
LAST = H - PS
HEADS, DQ, DV = 4, 16, 24
TOK = PS * PS
GROUP = 3
MLP = 192
PIX = H * W
BASE = 64


def start_semaphores(nc, semaphores):
    with nc.Block() as block:
        @block.gpsimd
        def _(pool):
            for s in semaphores:
                pool.sem_inc(s, BASE)


def constants():
    eye = np.eye(128, dtype=np.float32)
    centre = np.eye(C, dtype=np.float32) - np.float32(1.0 / C)
    group = np.zeros((C, C), np.float32)
    for g in range(C // GROUP):
        group[g * GROUP:(g + 1) * GROUP, g * GROUP:(g + 1) * GROUP] = 1.0 / GROUP
    head_rows = np.zeros((128, HEADS), np.float32)
    for h in range(HEADS):
        head_rows[32 * h:32 * h + 32, h] = 1.0
    one_rows = np.zeros((128, 1), np.float32)
    one_rows[DQ::32] = 1.0
    cols = np.ones((C, W), np.float32)
    for i in range(STEP, W + STEP - PS, STEP):
        top, down = (i, i + PS - STEP) if i + PS <= W else (W - PS, i + PS - STEP)
        cols[:, top:down] *= 0.5
    first_rows = np.full((C, NWIN), 0.5, np.float32)
    first_rows[:, 0] = 1.0
    return {"k_eye": eye, "k_centre": centre, "k_group": group, "k_head_rows": head_rows,
            "k_one_rows": one_rows, "k_cols": cols, "k_first_rows": first_rows}


def group_norm_statistics(nc, x, t):
    CH, PART, FM = 8192, 8, 512
    with ExitStack() as ctx:
        xin = ctx.enter_context(nc.sbuf_tensor("gn_xin", [C, 2, CH], F32))
        stats = ctx.enter_context(nc.sbuf_tensor("gn_stats", [C, B * PIX // FM, 6], F32))
        loaded = [ctx.enter_context(nc.semaphore(f"gn_loaded{i}")) for i in range(2)]
        read = ctx.enter_context(nc.semaphore("gn_read"))
        aggregated = ctx.enter_context(nc.semaphore("gn_aggregated"))
        block = ctx.enter_context(nc.Block())
        rows = H // PART
        steps = B * PART

        def part(m):
            b, q = m // PART, m % PART
            return x[bass.ds(b, 1), :, bass.ds(q * rows, rows), :].rearrange("a c r w -> (a c) (r w)")

        @block.sync
        def _(sp):
            for i in range(2):
                sp.dma_start(xin[:, i, :], part(i)).then_inc(loaded[i], 16)
            with sp.Fori(0, steps // 2 - 1) as s:
                for i in range(2):
                    sp.wait_ge(read, 2 * s + i + 1)
                    sp.dma_start(xin[:, i, :], part(2 * s + (i + 2))).then_inc(loaded[i], 16)

        @block.vector
        def _(dve):
            per = CH // FM
            with dve.Fori(0, steps // 2) as s:
                for i in range(2):
                    dve.wait_ge(loaded[i], 16 * s + 16)
                    for k in range(per):
                        last = dve.bn_stats(stats[:, bass.ds((2 * s + i) * per + k, 1), :].rearrange("p a b -> p (a b)"), xin[:, i, k * FM:(k + 1) * FM])
                    last.then_inc(read, 1)
            dve.wait_ge(read, steps)
            for b in range(B):
                n = PIX // FM
                dve.bn_aggr(t["mean_var"][:, b, :], stats[:, b * n:(b + 1) * n, :]).then_inc(aggregated, 1)
            dve.wait_ge(aggregated, B)


def attention_setup(nc, p, t):
    with ExitStack() as ctx:
        def sb(name, shape, dt=F32):
            return ctx.enter_context(nc.sbuf_tensor("as_" + name, shape, dt))
        m2 = sb("m2", [C, 2, B])
        avg = sb("avg", [C, 2, B])
        sq = sb("sq", [C, B])
        sd = sb("sd", [C, B])
        group = sb("group", [C, C])
        n1 = sb("n1", [C, 2])
        one_rows = sb("one_rows", [128, 1])
        bv = sb("bv", [C, 1])
        eps = sb("eps", [C, 1])
        ps = ctx.enter_context(nc.psum_tensor("as_ps", [128, 4, 512], F32))
        loaded = ctx.enter_context(nc.semaphore("as_loaded"))
        dch = ctx.enter_context(nc.semaphore("as_vector_done"))
        pch = ctx.enter_context(nc.semaphore("as_products_done"))
        ach = ctx.enter_context(nc.semaphore("as_roots_done"))
        cleared = ctx.enter_context(nc.semaphore("as_cleared"))
        block = ctx.enter_context(nc.Block())
        nload = 14

        @block.gpsimd
        def _(pool):
            pool.memset(t["wqk"][:], 0.0).then_inc(cleared, 1)
            pool.memset(t["mz"][:], 0.0).then_inc(cleared, 1)
            pool.memset(t["vaug"][:], 1.0).then_inc(cleared, 1)
            pool.memset(t["acc"][:], 0.0).then_inc(cleared, 1)
            pool.memset(t["eps5"][:], 1e-5).then_inc(cleared, 1)
            pool.memset(eps[:], 1e-5).then_inc(cleared, 1)
            pool.memset(t["ones"][:], 1.0 / C).then_inc(cleared, 1)
            pool.memset(t["zero"][:], 0.0).then_inc(cleared, 1)
            pool.memset(t["one"][:], 1.0).then_inc(cleared, 1)

        @block.sync
        def _(sp):
            sp.wait_ge(cleared, 9)
            for i, name in enumerate(("wq", "wk")):
                for h in range(HEADS):
                    sp.dma_start(t["wqk"][:, i, 32 * h:32 * h + DQ], p[name][:, h * DQ:(h + 1) * DQ]).then_inc(loaded, 16)
            sp.dma_start(t["wv"][:], p["wv"]).then_inc(loaded, 16)
            sp.dma_start(t["wproj"][:], p["wproj"]).then_inc(loaded, 16)
            sp.dma_start(n1[:, 0:1], p["norm1_w"].rearrange("(c a) -> c a", a=1)).then_inc(loaded, 16)
            sp.dma_start(n1[:, 1:2], p["norm1_b"].rearrange("(c a) -> c a", a=1)).then_inc(loaded, 16)
            sp.dma_start(group[:], p["k_group"]).then_inc(loaded, 16)
            sp.dma_start(one_rows[:], p["k_one_rows"]).then_inc(loaded, 16)
            for k in ("eye", "centre", "head_rows", "cols", "first_rows"):
                sp.dma_start(t[k][:], p["k_" + k]).then_inc(loaded, 16)

        nload += 5

        @block.scalar
        def _(act):
            act.wait_ge(dch, 4)
            act.activation(sd[:], sq[:], ACT.Sqrt, bias=eps[:]).then_inc(ach, 1)

        @block.tensor
        def _(pe):
            pe.wait_ge(loaded, 16 * nload)
            pe.wait_ge(dch, 2)
            pe.matmul(ps[0:C, 0, 0:2 * B], group[:], m2[:].rearrange("p a b -> p (a b)"), start=True, stop=True).then_inc(pch, 1)
            pe.matmul(ps[:, 1, 0:1], t["wqk"][:, 0, :], n1[:, 1:2], start=True, stop=True)
            pe.matmul(ps[:, 1, 1:2], t["wqk"][:, 1, :], n1[:, 1:2], start=True, stop=True)
            pe.matmul(ps[0:C, 1, 2:3], t["wv"][:], n1[:, 1:2], start=True, stop=True).then_inc(pch, 1)
            pe.wait_ge(dch, 6)
            pe.matmul(ps[0:C, 2, 0:1], t["wproj"][:], bv[:], start=True, stop=True)
            pe.wait_ge(dch, 9)
            pe.matmul(ps[0:C, 3, 0:B], t["centre"][:], t["gn_shift"][:], start=True, stop=True).then_inc(pch, 1)

        @block.vector
        def _(dve):
            n = [0]

            def link(ins):
                n[0] += 1
                ins.then_inc(dch, 1)
                dve.wait_ge(dch, n[0])

            mv = t["mean_var"]
            dve.wait_ge(loaded, 16 * nload)
            link(dve.tensor_tensor(m2[:, 1, :], mv[:, :, 0], mv[:, :, 0], ALU.mult))
            dve.tensor_copy(m2[:, 0, :], mv[:, :, 0])
            link(dve.tensor_tensor(m2[:, 1, :], m2[:, 1, :], mv[:, :, 1], ALU.add))
            dve.wait_ge(pch, 1)
            dve.tensor_copy(avg[:].rearrange("p a b -> p (a b)"), ps[0:C, 0, 0:2 * B]).then_inc(dch, 1)
            n[0] += 1
            dve.wait_ge(dch, n[0])
            dve.tensor_tensor(sq[:], avg[:, 0, :], avg[:, 0, :], ALU.mult).then_inc(ach, 1)
            dve.wait_ge(ach, 1)
            link(dve.tensor_tensor(sq[:], avg[:, 1, :], sq[:], ALU.subtract))
            dve.wait_ge(pch, 2)
            link(dve.tensor_scalar(t["qk_bias"][:, 0:1], ps[:, 1, 0:1], 0.25, None, ALU.mult))
            link(dve.tensor_copy(bv[:], ps[0:C, 1, 2:3]))
            link(dve.tensor_tensor(t["qk_bias"][:, 1:2], ps[:, 1, 1:2], one_rows[:], ALU.add))
            dve.wait_ge(ach, 2)
            link(dve.reciprocal(t["gn_scale"][:], sd[:]))
            link(dve.scalar_tensor_tensor(out=t["gn_shift"][:], in0=avg[:, 0, :], scalar=-1.0, in1=t["gn_scale"][:], op0=ALU.mult, op1=ALU.mult))
            dve.wait_ge(pch, 3)
            link(dve.tensor_copy(t["cen_shift"][:], ps[0:C, 3, 0:B]))
            for b in range(B):
                link(dve.tensor_tensor(t["out_shift"][:, b:b + 1], ps[0:C, 2, 0:1], t["gn_shift"][:, b:b + 1], ALU.add))
                link(dve.tensor_scalar(t["cen_w"][:, b, :], t["centre"][:], t["gn_scale"][:, b:b + 1], None, ALU.mult))
            link(dve.tensor_scalar(t["wqk"][:, 0, :], t["wqk"][:, 0, :], n1[:, 0:1], 0.25, ALU.mult, ALU.mult))
            link(dve.tensor_scalar(t["wqk"][:, 1, :], t["wqk"][:, 1, :], n1[:, 0:1], None, ALU.mult))
            link(dve.tensor_scalar(t["wv"][:], t["wv"][:], n1[:, 0:1], None, ALU.mult))
            link(dve.tensor_scalar(t["neg_eye"][:], t["eye"][:], -1.0, None, ALU.mult))


def attention(nc, x, x2, t, batches=B, bands=NWIN - 1):
    CK = 512
    NCK = PS * W // CK
    NT = PS * W // 128
    VW = DV + 1
    with ExitStack() as ctx:
        def sb(name, shape, dt=F32):
            return ctx.enter_context(nc.sbuf_tensor("at_" + name, shape, dt))

        sems = []

        def sem(name):
            sems.append(ctx.enter_context(nc.semaphore("at_" + name)))
            return sems[-1]

        xin = sb("xin", [C, PS * W])
        xg = sb("xg", [C, PS * W])
        y = sb("y", [C, PS * W])
        sq = sb("sq", [C, 2, CK])
        sd = sb("sd", [128, NT])
        rs = sb("rs", [128, NT])
        out = sb("out", [C, PS * W])
        win = sb("win", [C, 2, TOK])
        q = sb("q", [128, 2, TOK])
        k = sb("k", [128, 2, TOK])
        kz = sb("kz", [128, 2, HEADS, TOK])
        qaug = sb("qaug", [128, TOK])
        E = sb("E", [128, 2, HEADS, 2 * TOK])
        rden = sb("rden", [128, 8])
        on = sb("on", [128, 2, C])
        ot = sb("ot", [C, TOK])
        cen_w = sb("cen_w", [C, C])
        cen_shift = sb("cen_shift", [C, 1])
        scale = sb("scale", [C, 1])
        shift = sb("shift", [C, 1])
        psum = ctx.enter_context(nc.psum_tensor("at_ps", [128, 8, 512], F32))
        acc, vaug, mz = t["acc"], t["vaug"], t["mz"]
        qk_ps = psum[:, 4, :]
        vt_ps = psum[:, 5, :]
        pv_ps = psum[:, 6, :]
        pr_ps = psum[:, 7, :]
        qb = q[:].bitcast(BF16).rearrange("p b (n two) -> p b n two", two=2)[:, :, :, 1]
        kb = kz[:].bitcast(BF16).rearrange("p b h (n two) -> p b h n two", two=2)[:, :, :, :, 1]

        x_loaded, stored = (ctx.enter_context(nc.semaphore("at_" + name)) for name in ("x_loaded", "stored"))
        batch_set, xg_done = sem("batch_set"), sem("xg_done")
        cen_done, cs_done, sq_done, var_done = sem("cen_done"), sem("cs_done"), sem("sq_done"), sem("var_done")
        sd_done, rs_done, bc_done, y_done = sem("sd_done"), sem("rs_done"), sem("bc_done"), sem("y_done")
        win_ready, kz_ready = sem("win_ready"), sem("kz_ready")
        qk_done, v_done, s1_done, t_done, s2_done, pv_done, ot_done, proj_done = (
            sem(s) for s in ("qk_done", "v_done", "s1_done", "t_done", "s2_done", "pv_done", "ot_done", "proj_done"))
        qk_out, exp_done, ot_out = sem("qk_out"), sem("exp_done"), sem("ot_out")
        v_out, max_done, qaug_done, rden_done, norm_done, added = (
            sem(s) for s in ("v_out", "max_done", "qaug_done", "rden_done", "norm_done", "added"))
        weighted, acc_ready, out_done, out_half = sem("weighted"), sem("acc_ready"), sem("out_done"), sem("out_half")
        carried = sem("carried")
        start_semaphores(nc, sems)
        block = ctx.enter_context(nc.Block())

        def each_band(eng, body, start=None):
            with eng.Fori(0, batches) as b:
                if start is not None:
                    start(b)
                with eng.Fori(0, bands) as r:
                    body(b * (bands + 1) + r, r, False, b)
                body(b * (bands + 1) + bands, bands, True, b)

        def each_step(eng, n, step):
            base = n * NWIN
            for i in (0, 1):
                step(i, base + i, i)
            with eng.Fori(0, 7) as j:
                for u in range(2):
                    step(2 + u, base + 2 * j + (2 + u), 2 * j + (2 + u))
            for i in range(16, NWIN + 2):
                step(i, base + i, i)

        def column(w):
            return LAST if isinstance(w, int) and w == NWIN - 1 else w * STEP

        def window(a, w):
            return a[:].rearrange("p (r c) -> p r c", c=W)[:, :, bass.ds(column(w), PS)]

        @block.sync
        def _(sp):
            def body(n, r, last, b):
                sp.wait_ge(xg_done, BASE + n)
                row = LAST if last else r * STEP
                sp.dma_start(xin[:], x[bass.ds(b, 1), :, bass.ds(row, PS), :].rearrange("a c r w -> (a c) (r w)")).then_inc(x_loaded, 16)
            each_band(sp, body)

        @block.gpsimd
        def _(pool):
            def copy(to, of):
                one = t["one"][:]
                for _ in of.shape[2:]:
                    one = one.unsqueeze(1)
                return pool.tensor_tensor(to, of, one.to_broadcast(list(of.shape)), ALU.mult)

            def clear(to):
                z = t["zero"][:].to_broadcast([C, to.shape[1]])
                return pool.tensor_tensor(to, z, z, ALU.mult)

            def gather(i, Wd, w):
                pool.wait_ge(v_done, BASE + Wd - 1)
                copy(win[:, i % 2, :].rearrange("p (r c) -> p r c", c=PS), window(y, w)).then_inc(win_ready, 1)

            def mask(i, Wd):
                pool.wait_ge(qk_out, BASE + Wd + 1)
                for h in range(HEADS):
                    pool.wait_ge(s2_done, BASE + HEADS * (Wd - 2) + (h + 1))
                    pool.tensor_tensor(kz[:, i % 2, h, :], k[:, i % 2, :], t["head_rows"][:, h:h + 1].to_broadcast([128, TOK]),
                                       ALU.mult).then_inc(kz_ready, 1)

            def body(n, r, last, b):
                chain = b * (bands + 3) + r
                pool.wait_ge(weighted, BASE + n)
                if last:
                    pool.wait_ge(stored, 16 * n)
                    copy(out[:, 0:STEP * W], acc[:, 2 * W:]).then_inc(carried, 1)
                    pool.wait_ge(carried, BASE + chain + 1)
                    copy(acc[:, 0:STEP * W], out[:, 0:STEP * W]).then_inc(carried, 1)
                    pool.wait_ge(carried, BASE + chain + 2)
                    clear(acc[:, STEP * W:]).then_inc(acc_ready, 1)
                else:
                    copy(acc[:, 0:2 * W], acc[:, STEP * W:]).then_inc(carried, 1)
                    pool.wait_ge(carried, BASE + chain + 1)
                    clear(acc[:, 2 * W:]).then_inc(acc_ready, 1)
                pool.wait_ge(y_done, BASE + NCK * n + NCK)
                gather(0, n * NWIN, 0)
                gather(1, n * NWIN + 1, 1)
                mask(0, n * NWIN)

                def step(i, Wd, w):
                    if i < NWIN - 2:
                        gather(i + 2, Wd + 2, w + 2)
                    if i < NWIN - 1:
                        mask(i + 1, Wd + 1)
                each_step(pool, n, step)
                pool.wait_ge(out_half, BASE + n + 1)
                pool.wait_ge(xg_done, BASE + n + 1)
                pool.tensor_tensor(out[:], out[:], xg[:], ALU.add).then_inc(out_done, 1)
                if last:
                    clear(acc[:]).then_inc(carried, 1)
                    pool.wait_ge(carried, BASE + chain + 3)
                pool.wait_ge(out_done, BASE + n + 1)
                rows = PS if last else STEP
                row = LAST if last else r * STEP
                pool.dma_start(x2[bass.ds(b, 1), :, bass.ds(row, rows), :].rearrange("a c r w -> (a c) (r w)"),
                               out[:, 0:rows * W]).then_inc(stored, 16)
            each_band(pool, body)
            pool.wait_ge(stored, 16 * batches * (bands + 1))

        @block.scalar
        def _(act):
            def body(n, r, last, b):
                act.wait_ge(win_ready, BASE + n * NWIN)
                act.wait_ge(batch_set, BASE + 4 * b + 4)
                for c in range(NCK):
                    act.wait_ge(cen_done, BASE + NCK * n + c + 1)
                    act.activation(y[:, c * CK:(c + 1) * CK], psum[0:C, c % 4, :], ACT.Identity, bias=cen_shift[:]).then_inc(cs_done, 1)
                act.wait_ge(var_done, BASE + NCK * n + NCK)
                act.activation(sd[:], psum[:, 4, 0:NT], ACT.Sqrt, bias=t["eps5"][:]).then_inc(sd_done, 1)
                act.wait_ge(out_done, BASE + n)
                act.activation(xg[:], xin[:], ACT.Identity, bias=shift[:], scale=scale[:]).then_inc(xg_done, 1)

                def queries_and_keys(i, Wd):
                    act.wait_ge(qk_done, BASE + Wd + 1)
                    act.wait_ge(qaug_done, BASE + Wd - 1)
                    act.wait_ge(kz_ready, BASE + HEADS * (Wd - 1))
                    act.activation(q[:, i % 2, :], qk_ps[:, 0:TOK], ACT.Identity, bias=t["qk_bias"][:, 0:1])
                    act.activation(k[:, i % 2, :], qk_ps[:, TOK:], ACT.Identity, bias=t["qk_bias"][:, 1:2]).then_inc(qk_out, 1)

                def step(i, Wd, w):
                    W1, W2 = Wd - 1, Wd - 2

                    def exponential(h):
                        if 1 <= i <= NWIN:
                            if h == 0:
                                act.wait_ge(pv_done, BASE + W1 - 1)
                            act.wait_ge(s2_done, BASE + HEADS * W1 + (h + 1))
                            act.activation(E[:, (i - 1) % 2, h, :], psum[:, 2 + h % 2, :], ACT.Exp).then_inc(exp_done, 1)

                    exponential(0)
                    if i >= 2:
                        act.wait_ge(ot_done, BASE + W2 + 1)
                        act.wait_ge(proj_done, BASE + W2)
                        act.activation(ot[:], pr_ps[0:C, 0:TOK], ACT.Copy).then_inc(ot_out, 1)
                    exponential(1)
                    if i < NWIN - 1:
                        queries_and_keys(i + 1, Wd + 1)
                    exponential(2)
                    exponential(3)

                queries_and_keys(0, n * NWIN)
                each_step(act, n, step)
            each_band(act, body)

        @block.tensor
        def _(pe):
            def body(n, r, last, b):
                pe.wait_ge(qk_out, BASE + n * NWIN)
                pe.wait_ge(exp_done, BASE + n * (HEADS * NWIN))
                pe.wait_ge(max_done, BASE + n * (HEADS * NWIN))
                pe.wait_ge(batch_set, BASE + 4 * b + 4)
                pe.wait_ge(x_loaded, 16 * n + 16)

                def variance(c):
                    pe.wait_ge(sq_done, BASE + NCK * n + c + 1)
                    for s in range(CK // 128):
                        m = pe.matmul(psum[:, 4, 4 * c + s:4 * c + s + 1], sq[:, c % 2, 128 * s:128 * s + 128], t["ones"][:],
                                      start=True, stop=True)
                    m.then_inc(var_done, 1)

                for c in range(NCK):
                    if c >= 4:
                        pe.wait_ge(cs_done, BASE + NCK * n + c - 3)
                    pe.matmul(psum[0:C, c % 4, :], cen_w[:], xin[:, c * CK:(c + 1) * CK], start=True, stop=True).then_inc(cen_done, 1)
                    if c >= 1:
                        variance(c - 1)
                variance(NCK - 1)
                pe.wait_ge(rs_done, BASE + n + 1)
                for c in range(NCK):
                    if c >= 2:
                        pe.wait_ge(y_done, BASE + NCK * n + c - 1)
                    for s in range(CK // 128):
                        m = pe.matmul(psum[0:C, 5 + c % 2, 128 * s:128 * s + 128],
                                      rs[:, 4 * c + s:4 * c + s + 1].to_broadcast([128, C]), t["eye"][:], start=True, stop=True)
                    m.then_inc(bc_done, 1)
                pe.wait_ge(y_done, BASE + NCK * n + NCK)

                def queries_and_keys(i, Wd):
                    pe.wait_ge(win_ready, BASE + Wd + 1)
                    pe.wait_ge(qk_out, BASE + Wd)
                    for z in range(2):
                        m = pe.matmul(qk_ps[:, z * TOK:(z + 1) * TOK], t["wqk"][:, z, :], win[:, i % 2, :], start=True, stop=True)
                    m.then_inc(qk_done, 1)

                def step(i, Wd, w):
                    W1, W2 = Wd - 1, Wd - 2
                    has0, has1, has2 = i < NWIN, 1 <= i <= NWIN, i >= 2
                    b0, b1 = i % 2, (i - 1) % 2

                    def scores_for_max(h):
                        if not has0:
                            return
                        pe.wait_ge(kz_ready, BASE + HEADS * Wd + (h + 1))
                        pe.wait_ge(max_done, BASE + HEADS * Wd + (h - 1))
                        for j in range(2):
                            m = pe.matmul(psum[:, h % 2, TOK * j:TOK * j + TOK], qb[:, b0, 128 * j:128 * j + 128],
                                          kb[:, b0, h, :], start=True, stop=True)
                        m.then_inc(s1_done, 1)

                    def scores(h):
                        if not has1:
                            return
                        pe.wait_ge(exp_done, BASE + HEADS * W1 + (h - 1))
                        for j in range(2):
                            m = pe.matmul(psum[:, 2 + h % 2, TOK * j:TOK * j + TOK],
                                          kz[:, b1, h, 128 * j:128 * j + 128], qaug[:], start=True, stop=True)
                        m.then_inc(s2_done, 1)

                    def values(h):
                        if not has1:
                            return
                        pe.wait_ge(exp_done, BASE + HEADS * W1 + (h + 1))
                        for j in range(2):
                            o = (j * HEADS + h) * VW
                            for z in range(2):
                                e = z * TOK + 128 * j
                                m = pe.matmul(pv_ps[:, o:o + VW], E[:, b1, h, e:e + 128], vaug[:, b1, z, h, :],
                                              start=(z == 0), stop=(z == 1))
                        if h == HEADS - 1:
                            m.then_inc(pv_done, 1)

                    scores_for_max(0)
                    if has0:
                        pe.wait_ge(qaug_done, BASE + Wd)
                        for j in range(2):
                            m = pe.matmul(vt_ps[:, j * C:(j + 1) * C], win[:, b0, 128 * j:128 * j + 128], t["wv"][:], start=True, stop=True)
                        m.then_inc(v_done, 1)
                    if has1:
                        pe.wait_ge(qaug_done, BASE + W1 + 1)
                    scores(0)
                    scores_for_max(1)
                    if has2:
                        pe.wait_ge(norm_done, BASE + W2 + 1)
                        pe.wait_ge(added, BASE + W2)
                        for j in range(2):
                            m = pe.matmul(pr_ps[0:C, 128 * j:128 * j + 128], on[:, j, :], t["eye"][:], start=True, stop=True)
                        m.then_inc(ot_done, 1)
                    scores(1)
                    scores_for_max(2)
                    if i < NWIN - 1:
                        queries_and_keys(i + 1, Wd + 1)
                    scores(2)
                    scores_for_max(3)
                    if has2:
                        pe.wait_ge(ot_out, BASE + W2 + 1)
                        pe.matmul(pr_ps[0:C, 0:TOK], t["wproj"][:], ot[:], start=True, stop=True).then_inc(proj_done, 1)
                    if has1:
                        pe.wait_ge(norm_done, BASE + W1)
                    values(0)
                    scores(3)
                    values(1)
                    if has0:
                        pe.wait_ge(max_done, BASE + HEADS * Wd + HEADS)
                        pe.wait_ge(v_out, BASE + Wd + 1)
                        for j in range(2):
                            m = pe.matmul(vt_ps[:, 128 * j:128 * j + 128], mz[:, b0, j, :], t["neg_eye"][:], start=True, stop=True)
                        m.then_inc(t_done, 1)
                    values(2)
                    values(3)

                queries_and_keys(0, n * NWIN)
                each_step(pe, n, step)
            each_band(pe, body)

        @block.vector
        def _(dve):
            def start(b):
                dve.wait_ge(xg_done, BASE + b * (bands + 1))
                dve.tensor_copy(cen_w[:], t["cen_w"][:, bass.ds(b, 1), :].rearrange("p a c -> p (a c)")).then_inc(batch_set, 1)
                for to, of in ((cen_shift, "cen_shift"), (scale, "gn_scale"), (shift, "out_shift")):
                    dve.tensor_copy(to[:], t[of][:, bass.ds(b, 1)]).then_inc(batch_set, 1)

            def body(n, r, last, b):
                for c in range(NCK):
                    dve.wait_ge(cs_done, BASE + NCK * n + c + 1)
                    if c >= 2:
                        dve.wait_ge(var_done, BASE + NCK * n + c - 1)
                    yc = y[:, c * CK:(c + 1) * CK]
                    dve.tensor_tensor(sq[:, c % 2, :], yc, yc, ALU.mult).then_inc(sq_done, 1)
                dve.wait_ge(sd_done, BASE + n + 1)
                dve.reciprocal(rs[:], sd[:]).then_inc(rs_done, 1)
                for c in range(NCK):
                    dve.wait_ge(bc_done, BASE + NCK * n + c + 1)
                    yc = y[:, c * CK:(c + 1) * CK]
                    dve.tensor_tensor(yc, psum[0:C, 5 + c % 2, :], yc, ALU.mult).then_inc(y_done, 1)

                def maxima(i, h, Wd):
                    dve.wait_ge(s1_done, BASE + HEADS * Wd + (h + 1))
                    dve.tensor_reduce(mz[:, i % 2, :, 32 * h + DQ], psum[:, h % 2, :].rearrange("p (j m) -> p j m", m=TOK),
                                      AX.X, ALU.max).then_inc(max_done, 1)

                def step(i, Wd, w):
                    W1, W2 = Wd - 1, Wd - 2
                    if i < NWIN:
                        dve.wait_ge(t_done, BASE + Wd - 1)
                        maxima(i, 0, Wd)
                        dve.wait_ge(v_done, BASE + Wd + 1)
                        dve.wait_ge(pv_done, BASE + Wd - 1)
                        dve.tensor_copy(vaug[:, i % 2, :, :, 0:DV].rearrange("p j h d -> p (j h) d"),
                                        vt_ps[:, 0:2 * C].rearrange("p (a d) -> p a d", d=DV)).then_inc(v_out, 1)
                        for h in range(1, HEADS):
                            maxima(i, h, Wd)
                    if i >= 2:
                        if i == 2:
                            dve.wait_ge(acc_ready, BASE + n + 1)
                        dve.wait_ge(proj_done, BASE + W2 + 1)
                        a = window(acc, w - 2)
                        dve.tensor_tensor(a, pr_ps[0:C, 0:TOK].rearrange("p (r c) -> p r c", c=PS), a, ALU.add).then_inc(added, 1)
                    if i < NWIN:
                        dve.wait_ge(t_done, BASE + Wd + 1)
                        dve.tensor_tensor(qaug[:], vt_ps[:, 0:TOK], q[:, i % 2, :], ALU.add).then_inc(qaug_done, 1)
                    if 1 <= i <= NWIN:
                        dve.wait_ge(pv_done, BASE + W1 + 1)
                        o = pv_ps[:, 0:8 * VW].rearrange("p (a d) -> p a d", d=VW)
                        dve.reciprocal(rden[:], o[:, :, DV]).then_inc(rden_done, 1)
                        dve.wait_ge(rden_done, BASE + W1 + 1)
                        dve.tensor_tensor(on[:].rearrange("p j (h d) -> p (j h) d", d=DV), o[:, :, 0:DV],
                                          rden[:].unsqueeze(2).to_broadcast([128, 8, DV]), ALU.mult).then_inc(norm_done, 1)
                each_step(dve, n, step)
                dve.wait_ge(added, BASE + (n + 1) * NWIN)
                dve.wait_ge(stored, 16 * n)
                dve.tensor_tensor(out[:].rearrange("p (r w) -> p r w", w=W), acc[:].rearrange("p (r w) -> p r w", w=W),
                                  t["cols"][:].unsqueeze(1).to_broadcast([C, PS, W]), ALU.mult).then_inc(weighted, 1)
                dve.wait_ge(weighted, BASE + n + 1)
                if last:
                    dve.tensor_scalar(out[:, 0:STEP * W], out[:, 0:STEP * W], 0.5, None, ALU.mult).then_inc(out_half, 1)
                else:
                    dve.tensor_scalar(out[:, 0:2 * W], out[:, 0:2 * W], t["first_rows"][:, bass.ds(r, 1)], None, ALU.mult).then_inc(out_half, 1)
            each_band(dve, body, start)


def attention_tables(nc, ctx):
    shapes = {"mean_var": ([C, B, 2], F32), "wqk": ([C, 2, 128], F32), "wv": ([C, C], F32), "wproj": ([C, C], F32),
              "eye": ([128, 128], F32), "neg_eye": ([128, 128], BF16), "centre": ([C, C], F32), "head_rows": ([128, HEADS], F32),
              "cols": ([C, W], F32), "first_rows": ([C, NWIN], F32), "ones": ([C, 1], F32), "zero": ([C, 1], F32), "one": ([C, 1], F32), "eps5": ([128, 1], F32),
              "qk_bias": ([128, 2], F32), "gn_scale": ([C, B], F32), "gn_shift": ([C, B], F32), "cen_shift": ([C, B], F32),
              "out_shift": ([C, B], F32), "cen_w": ([C, B, C], F32), "mz": ([128, 2, 2, 128], BF16),
              "vaug": ([128, 2, 2, HEADS, DV + 1], F32), "acc": ([C, PS * W], F32)}
    return {k: ctx.enter_context(nc.sbuf_tensor("t_" + k, s, d)) for k, (s, d) in shapes.items()}
CHK = 512
FG = 16
BLK = 32
OWN = 28
NBLK = 9
TAPS = 5
CPB = 128 // BLK
NGRP = MLP // CPB
UR = OWN // 2


def conv_constants():
    taps = np.zeros((128, TAPS, 128), np.float32)
    for c in range(CPB):
        for m in range(BLK):
            for dy in range(TAPS):
                k = m + dy - TAPS // 2
                if 0 <= k < BLK:
                    taps[c * BLK + k, dy, c * BLK + m] = 1.0
    return {"k_taps": taps}


def fc1(nc, p, x2, ydr, groups=B * H // FG):
    NTOK = FG * W
    NCK = NTOK // CHK
    NT = NTOK // 128
    with ExitStack() as ctx:
        def sb(name, shape, dt=F32):
            return ctx.enter_context(nc.sbuf_tensor("f1_" + name, shape, dt))

        def sem(name):
            return ctx.enter_context(nc.semaphore("f1_" + name))

        w1 = sb("w1", [C, MLP])
        n2 = sb("n2", [C, 2])
        b1 = sb("b1", [C, 2])
        bias = sb("bias", [C, 2])
        eye = sb("eye", [128, 128])
        centre = sb("centre", [C, C])
        ones = sb("ones", [C, 1])
        eps = sb("eps", [128, 1])
        xin = sb("xin", [C, 2, NTOK])
        z = sb("z", [C, 2, NTOK])
        sq = sb("sq", [C, 2, CHK])
        sd = sb("sd", [128, NT])
        rs = sb("rs", [128, NT])
        yo = sb("yo", [C, 4, 2, CHK])
        psum = ctx.enter_context(nc.psum_tensor("f1_ps", [128, 8, 512], F32))
        w_loaded, filled, w_set, b_done = sem("w_loaded"), sem("filled"), sem("w_set"), sem("b_done")
        x_loaded = [sem(f"x_loaded{i}") for i in range(2)]
        stored = [sem(f"stored{i}") for i in range(4)]
        cen_done, cs_done, sq_done, var_done, sd_done, rs_done, bc_done, z_done, f_done, y_done = (
            sem(s) for s in ("cen_done", "cs_done", "sq_done", "var_done", "sd_done", "rs_done", "bc_done", "z_done", "f_done", "y_done"))
        block = ctx.enter_context(nc.Block())
        per = H // FG

        def steps(eng, step):
            step(0, 0, True, False)
            with eng.Fori(0, (groups - 2) // 2) as j:
                step(1, 2 * j + 1, True, True)
                step(0, 2 * j + 2, True, True)
            step(1, groups - 1, True, True)
            step(0, groups, False, True)

        def rows_of(a, k):
            return a[bass.ds(k // per, 1), :, bass.ds((k % per) * FG, FG), :].rearrange("a c r w -> (a c) (r w)")

        @block.gpsimd
        def _(pool):
            pool.memset(ones[:], 1.0 / C).then_inc(filled, 1)
            pool.memset(eps[:], 1e-5).then_inc(filled, 1)
            with pool.Fori(0, groups) as k:
                for c in range(NCK):
                    pool.wait_ge(y_done, k * NCK + (c + 1))
                    dst = ydr[:, bass.ds((k % per) * FG + 2 * c, 2), bass.ds(k // per, 1), :]
                    for h in range(2):
                        pool.dma_start(dst[h * C:(h + 1) * C].rearrange("c r b w -> c r (b w)"),
                                       yo[:, c % 4, h, :].rearrange("c (r w) -> c r w", w=W)).then_inc(stored[c % 4], 16)
            for i in range(4):
                pool.wait_ge(stored[i], 64 * groups)

        @block.sync
        def _(sp):
            sp.dma_start(w1[:], p["fc1_w"]).then_inc(w_loaded, 16)
            sp.dma_start(n2[:, 0:1], p["norm2_w"].rearrange("(c a) -> c a", a=1)).then_inc(w_loaded, 16)
            sp.dma_start(n2[:, 1:2], p["norm2_b"].rearrange("(c a) -> c a", a=1)).then_inc(w_loaded, 16)
            for h in range(2):
                sp.dma_start(b1[:, h:h + 1], p["fc1_b"][h * C:(h + 1) * C].rearrange("(c a) -> c a", a=1)).then_inc(w_loaded, 16)
            sp.dma_start(eye[:], p["k_eye"]).then_inc(w_loaded, 16)
            sp.dma_start(centre[:], p["k_centre"]).then_inc(w_loaded, 16)
            for i in range(2):
                sp.dma_start(xin[:, i, :], rows_of(x2, i)).then_inc(x_loaded[i], 16)
            with sp.Fori(0, groups // 2 - 1) as j:
                for u in range(2):
                    k = 2 * j + u
                    sp.wait_ge(cen_done, k * NCK + NCK)
                    sp.dma_start(xin[:, u, :], rows_of(x2, 2 * j + (u + 2))).then_inc(x_loaded[u], 16)

        @block.tensor
        def _(pe):
            pe.wait_ge(w_loaded, 16 * 7)
            pe.wait_ge(filled, 2)
            for h in range(2):
                m = pe.matmul(psum[0:C, 3, h:h + 1], w1[:, h * C:(h + 1) * C], n2[:, 1:2], start=True, stop=True)
            m.then_inc(b_done, 1)
            pe.wait_ge(w_set, 2)

            def step(u, k, stats, products):
                base, was = k * NCK, (k - 1) * NCK
                o = 1 - u

                def variance(c):
                    pe.wait_ge(sq_done, base + (c + 1))
                    if c == 0:
                        pe.wait_ge(sd_done, k)
                    for s in range(CHK // 128):
                        m = pe.matmul(psum[:, 2, 4 * c + s:4 * c + s + 1], sq[:, c % 2, 128 * s:128 * s + 128], ones[:], start=True, stop=True)
                    m.then_inc(var_done, 1)

                def product(c):
                    pe.wait_ge(z_done, was + (c + 1))
                    for h in range(2):
                        bank = 4 + 2 * (c % 2) + h
                        m = pe.matmul(psum[0:C, bank, :], w1[:, h * C:(h + 1) * C], z[:, o, c * CHK:(c + 1) * CHK], start=True, stop=True)
                    m.then_inc(f_done, 1)

                if stats:
                    pe.wait_ge(x_loaded[u], 8 * (k - u) + 16)
                for c in range(NCK):
                    if stats:
                        if c >= 2 or products:
                            pe.wait_ge(cs_done, base + (c - 1))
                        pe.matmul(psum[0:C, c % 2, :], centre[:], xin[:, u, c * CHK:(c + 1) * CHK], start=True, stop=True).then_inc(cen_done, 1)
                        if c >= 1:
                            variance(c - 1)
                    if products:
                        if c == 0:
                            pe.wait_ge(rs_done, k)
                            pe.wait_ge(z_done, was)
                        else:
                            pe.wait_ge(z_done, was + c)
                        for s in range(CHK // 128):
                            m = pe.matmul(psum[0:C, 3, 128 * s:128 * s + 128], rs[:, 4 * c + s:4 * c + s + 1].to_broadcast([128, C]), eye[:],
                                          start=True, stop=True)
                        m.then_inc(bc_done, 1)
                        if c >= 1:
                            pe.wait_ge(y_done, was + max(c - 2, 0))
                            product(c - 1)
                if stats:
                    variance(NCK - 1)
                if products:
                    pe.wait_ge(y_done, was + (NCK - 2))
                    product(NCK - 1)
            steps(pe, step)

        @block.scalar
        def _(act):
            def step(u, k, stats, products):
                base, was = k * NCK, (k - 1) * NCK

                def gelu(c):
                    act.wait_ge(f_done, was + (c + 1))
                    act.wait_ge(stored[c % 4], 64 * (k - 1) + 32 * (c // 4))
                    for h in range(2):
                        i = act.activation(yo[:, c % 4, h, :], psum[0:C, 4 + 2 * (c % 2) + h, :], ACT.Gelu, bias=bias[:, h:h + 1])
                    i.then_inc(y_done, 1)

                for c in range(NCK):
                    if stats:
                        act.wait_ge(cen_done, base + (c + 1))
                        act.activation(z[:, u, c * CHK:(c + 1) * CHK], psum[0:C, c % 2, :], ACT.Copy).then_inc(cs_done, 1)
                    if products and c >= 1:
                        gelu(c - 1)
                if products:
                    gelu(NCK - 1)
                if stats:
                    act.wait_ge(var_done, base + NCK)
                    act.activation(sd[:], psum[:, 2, 0:NT], ACT.Sqrt, bias=eps[:]).then_inc(sd_done, 1)
            act.wait_ge(filled, 2)
            steps(act, step)

        @block.vector
        def _(dve):
            dve.wait_ge(b_done, 1)
            dve.wait_ge(w_loaded, 16 * 7)
            dve.tensor_tensor(bias[:], psum[0:C, 3, 0:2], b1[:], ALU.add).then_inc(w_set, 1)
            dve.tensor_scalar(w1[:], w1[:], n2[:, 0:1], None, ALU.mult).then_inc(w_set, 1)

            def step(u, k, stats, products):
                base, was = k * NCK, (k - 1) * NCK
                for c in range(NCK):
                    if stats:
                        dve.wait_ge(cs_done, base + (c + 1))
                        if c >= 2 or products:
                            dve.wait_ge(var_done, base + (c - 1))
                        zc = z[:, u, c * CHK:(c + 1) * CHK]
                        dve.tensor_tensor(sq[:, c % 2, :], zc, zc, ALU.mult).then_inc(sq_done, 1)
                    if products:
                        dve.wait_ge(bc_done, was + (c + 1))
                        zc = z[:, 1 - u, c * CHK:(c + 1) * CHK]
                        dve.tensor_tensor(zc, psum[0:C, 3, :], zc, ALU.mult).then_inc(z_done, 1)
                if stats:
                    dve.wait_ge(sd_done, k + 1)
                    if products:
                        dve.wait_ge(bc_done, base)
                    dve.reciprocal(rs[:], sd[:]).then_inc(rs_done, 1)
            steps(dve, step)


def conv(nc, p, ydr, sdr, pairs=NGRP // 2):
    with ExitStack() as ctx:
        def sb(name, shape, dt=F32):
            return ctx.enter_context(nc.sbuf_tensor("cv_" + name, shape, dt))

        def sem(name):
            return ctx.enter_context(nc.semaphore("cv_" + name))

        NS = 3
        PAD = TAPS // 2
        taps = sb("taps", [128, TAPS, 128])
        wd = sb("wd", [128, NGRP + 1, TAPS * TAPS])
        bd = sb("bd", [128, NGRP + 1])
        bcur = sb("bcur", [128, 2])
        band = sb("band", [128, 2, TAPS, 128])
        part = sb("part", [128, TAPS, 128])
        yin = sb("yin", [128, NS, B, W + 2 * PAD])
        gl = sb("gl", [128, NS, B * W])
        so = sb("so", [128, NS, B * W])
        psum = ctx.enter_context(nc.psum_tensor("cv_ps", [128, NS, 512], F32))
        w_loaded, filled, chain = sem("w_loaded"), sem("filled"), sem("chain")
        loaded = [sem(f"loaded{i}") for i in range(NS)]
        stored = [sem(f"stored{i}") for i in range(NS)]
        conv_done, gl_done = sem("conv_done"), sem("gl_done")
        summed = sem("summed")
        block = ctx.enter_context(nc.Block())
        SPB = 2 * NBLK
        SPS = SPB // NS
        LINKS = 2 * TAPS - 1

        def steps(eng, step):
            with eng.Fori(0, pairs) as j:
                for gg in range(2):
                    for t in range(NBLK):
                        step(j, gg, t, gg * NBLK + t)

        @block.sync
        def _(sp):
            sp.dma_start(taps[:], p["k_taps"]).then_inc(w_loaded, 16)
            sp.wait_ge(filled, 2)
            for c in range(CPB):
                rows = slice(c * BLK, (c + 1) * BLK)
                sp.dma_start(wd[rows, 0:NGRP, :], p["dw_w"].rearrange("(g c) a u v -> c a g (u v)", c=CPB)[c].to_broadcast([BLK, NGRP, TAPS * TAPS])
                             ).then_inc(w_loaded, 16)
                sp.dma_start(bd[rows, 0:NGRP], p["dw_b"].rearrange("(g c a) -> c a g", c=CPB, a=1)[c].to_broadcast([BLK, NGRP]),
                             allow_slow_non_contiguous=True).then_inc(w_loaded, 16)

            def step(j, gg, t, s):
                b = s % NS
                sp.wait_ge(summed, j * SPB + (s + 1))
                src = ydr[bass.ds(j * (2 * CPB) + gg * CPB, CPB), t * OWN:t * OWN + BLK]
                for i in range(B):
                    sp.dma_start(yin[:, b, i, PAD:PAD + W], src[:, :, i, :]).then_inc(loaded[b], 16)
            steps(sp, step)

        @block.gpsimd
        def _(pool):
            pool.memset(wd[:, NGRP, :], 0.0).then_inc(filled, 1)
            pool.memset(bd[:, NGRP:], 0.0).then_inc(filled, 1)

            def step(j, gg, t, s):
                pool.wait_ge(summed, j * SPB + (s + 1 + NS))
                dst = sdr[t, bass.ds(j * (2 * CPB) + gg * CPB, CPB)]
                pool.dma_start(dst.rearrange("c k b w -> (c k) (b w)"), so[:, s % NS, :]).then_inc(stored[s % NS], 16)
            steps(pool, step)
            for i in range(NS):
                pool.wait_ge(stored[i], 16 * pairs * SPS)

        @block.tensor
        def _(pe):
            def step(j, gg, t, s):
                b = s % NS
                if t == 0:
                    pe.wait_ge(chain, j * (2 * LINKS) + (gg + 1) * LINKS)
                pe.wait_ge(loaded[b], j * (32 * SPS) + 32 * (s // NS + 1))
                for dx in range(TAPS):
                    m = pe.matmul(psum[:, b, :], band[:, gg, dx, :], yin[:, b, :, dx:dx + W], start=(dx == 0), stop=(dx == TAPS - 1))
                m.then_inc(conv_done, 1)
            steps(pe, step)

        @block.scalar
        def _(act):
            def step(j, gg, t, s):
                b = s % NS
                act.wait_ge(conv_done, j * SPB + (s + 1))
                act.activation(gl[:, b, :], psum[:, b, :], ACT.Gelu, bias=bcur[:, gg:gg + 1]).then_inc(gl_done, 1)
            steps(act, step)

        @block.vector
        def _(dve):
            for i in range(NS):
                dve.memset(yin[:, i, :, 0:PAD], 0.0)
                dve.memset(yin[:, i, :, PAD + W:], 0.0).then_inc(summed, 1)
            dve.wait_ge(w_loaded, 16 * (2 * CPB + 1))

            def set_band(g, to, done):
                dve.tensor_scalar(bcur[:, to:to + 1], bd[:, bass.ds(g, 1)], 0.0, None, ALU.add)
                for dy in range(TAPS):
                    tap = taps[:, dy, :].unsqueeze(1).to_broadcast([128, TAPS, 128])
                    w = wd[:, bass.ds(g, 1), dy * TAPS:(dy + 1) * TAPS].rearrange("p a u -> p (a u)").unsqueeze(2).to_broadcast([128, TAPS, 128])
                    if dy:
                        dve.wait_ge(chain, done + (2 * dy - 1))
                    dve.tensor_tensor(part[:] if dy else band[:, to], tap, w, ALU.mult).then_inc(chain, 1)
                    if dy:
                        dve.wait_ge(chain, done + 2 * dy)
                        dve.tensor_tensor(band[:, to], band[:, to], part[:], ALU.add).then_inc(chain, 1)

            set_band(0, 0, 0)

            def step(j, gg, t, s):
                b = s % NS
                if t == 1:
                    dve.wait_ge(conv_done, j * SPB + gg * NBLK)
                    set_band(j * 2 + (gg + 1), 1 - gg, j * (2 * LINKS) + (gg + 1) * LINKS)
                dve.wait_ge(gl_done, j * SPB + (s + 1))
                dve.wait_ge(stored[b], j * (16 * SPS) + 16 * (s // NS))
                dve.tensor_tensor(so[:, b, :].rearrange("p (i w) -> p i w", w=W), gl[:, b, :].rearrange("p (i w) -> p i w", w=W),
                                  yin[:, b, :, PAD:PAD + W], ALU.add).then_inc(summed, 1)
            steps(dve, step)


def fc2(nc, p, x, x2, sdr, x1, tab, edges, batches=B, blocks=NBLK):
    rows = 2 if edges else UR
    n_ck = 2 * B if edges else rows * W // CHK
    NTOK = n_ck * CHK
    name = "fe_" if edges else "f2_"
    with ExitStack() as ctx:
        def sb(nm, shape, dt=F32):
            return ctx.enter_context(nc.sbuf_tensor(name + nm, shape, dt))

        def sem(nm):
            return ctx.enter_context(nc.semaphore(name + nm))

        NB = 1 if edges else 2
        w2 = sb("w2", [C, 2, C])
        b2 = sb("b2", [C, 1])
        st = sb("st", [C, NB, 2, NTOK])
        xa = sb("xa", [C, NB, NTOK])
        xb = sb("xb", [C, NB, NTOK])
        psum = ctx.enter_context(nc.psum_tensor(name + "ps", [128, n_ck, 512], F32))
        w_loaded = sem("w_loaded")
        loaded = [sem(f"loaded{i}") for i in range(NB)]
        stored = [sem(f"stored{i}") for i in range(NB)]
        xs_done, f_done, sums_done, squares_done = sem("xs_done"), sem("f_done"), sem("sums_done"), sem("squares_done")
        x1_done = sem("x1_done")
        block = ctx.enter_context(nc.Block())
        count = 1 if edges else batches * blocks * 2
        side = [(b, e) for b in range(B) for e in range(2)]

        def units(eng, unit):
            if edges:
                unit(0, 0, None, None)
                return
            with eng.Fori(0, batches * blocks) as i:
                for u in range(2):
                    unit(2 * i + u, u, i // blocks, i % blocks)

        def image(a, b, t, u):
            return a[bass.ds(b, 1), :, bass.ds(t * OWN + (2 + UR * u), UR), :].rearrange("a c r w -> (a c) (r w)")

        @block.sync
        def _(sp):
            sp.dma_start(w2[:], p["fc2_w"].rearrange("(h c) o -> c h o", h=2)).then_inc(w_loaded, 16)
            sp.dma_start(b2[:], p["fc2_b"].rearrange("(c a) -> c a", a=1)).then_inc(w_loaded, 16)

            def unit(n, u, b, t):
                if edges:
                    for i, (b, e) in enumerate(side):
                        at = slice(i * CHK, (i + 1) * CHK)
                        r0, k0, tt = (H - 2, BLK - 2, NBLK - 1) if e else (0, 0, 0)
                        for h in range(2):
                            sp.dma_start(st[:, 0, h, at].rearrange("c (r w) -> c r w", w=W), sdr[tt, h * C:(h + 1) * C, k0:k0 + 2, b, :]).then_inc(loaded[0], 16)
                        sp.dma_start(xa[:, 0, at], x2[b, :, r0:r0 + 2, :].rearrange("c r w -> c (r w)")).then_inc(loaded[0], 16)
                        sp.dma_start(xb[:, 0, at], x[b, :, r0:r0 + 2, :].rearrange("c r w -> c (r w)")).then_inc(loaded[0], 16)
                    return
                sp.wait_ge(stored[u], 8 * (n - u))
                for h in range(2):
                    src = sdr[bass.ds(t, 1), h * C:(h + 1) * C, 2 + UR * u:2 + UR * (u + 1), bass.ds(b, 1), :]
                    sp.dma_start(st[:, u, h, :].rearrange("c (r w) -> c r w", w=W), src.rearrange("a c r b w -> (a c) r (b w)")).then_inc(loaded[u], 16)
                sp.dma_start(xa[:, u, :], image(x2, b, t, u)).then_inc(loaded[u], 16)
                sp.dma_start(xb[:, u, :], image(x, b, t, u)).then_inc(loaded[u], 16)
            units(sp, unit)

        n_loads = 16 if edges else 4

        def wait_loaded(eng, n, u):
            eng.wait_ge(loaded[u], (n - u) * (8 * n_loads) + 16 * n_loads)

        @block.gpsimd
        def _(pool):
            def unit(n, u, b, t):
                wait_loaded(pool, n, u)
                pool.tensor_tensor(xa[:, u, :], xa[:, u, :], xb[:, u, :], ALU.add).then_inc(xs_done, 1)
            units(pool, unit)

        @block.tensor
        def _(pe):
            pe.wait_ge(w_loaded, 32)

            def unit(n, u, b, t):
                wait_loaded(pe, n, u)
                for c in range(n_ck):
                    pe.wait_ge(x1_done, n * n_ck + (c + 1))
                    for h in range(2):
                        m = pe.matmul(psum[0:C, c, :], w2[:, h, :], st[:, u, h, c * CHK:(c + 1) * CHK], start=(h == 0), stop=(h == 1))
                    m.then_inc(f_done, 1)
            units(pe, unit)

        @block.vector
        def _(dve):
            dve.sem_inc(x1_done, n_ck)
            dve.wait_ge(w_loaded, 32)

            def unit(n, u, b, t):
                dve.wait_ge(xs_done, n + 1)
                for c in range(n_ck):
                    dve.wait_ge(f_done, n * n_ck + (c + 1))
                    xc = xa[:, u, c * CHK:(c + 1) * CHK]
                    dve.scalar_tensor_tensor(out=xc, in0=psum[0:C, c, :], scalar=b2[:, 0:1], in1=xc, op0=ALU.add, op1=ALU.add).then_inc(x1_done, 1)
                dve.wait_ge(x1_done, n * n_ck + 2 * n_ck)
                sums = tab["row_sums"]
                if edges:
                    for i, (b, e) in enumerate(side):
                        r0 = b * H + (H - 2 if e else 0)
                        dve.tensor_reduce(sums[:, r0:r0 + 2, :], xa[:, 0, i * CHK:(i + 1) * CHK].rearrange("c (r q w) -> c r q w", r=2, w=64),
                                          AX.X, ALU.add).then_inc(sums_done, 1)
                else:
                    dve.tensor_reduce(sums[:, bass.ds(b * H + t * OWN + (2 + UR * u), UR), :],
                                      xa[:, u, :].rearrange("c (r q w) -> c r q w", q=4, w=64), AX.X, ALU.add).then_inc(sums_done, 1)
            units(dve, unit)

        @block.scalar
        def _(act):
            def unit(n, u, b, t):
                act.wait_ge(x1_done, n * n_ck + 2 * n_ck)
                if edges:
                    for i, (b, e) in enumerate(side):
                        at = slice(i * CHK, (i + 1) * CHK)
                        act.activation(xb[:, 0, at], xa[:, 0, at], ACT.Square,
                                       accum_out=tab["squares"][:, b, 2 * NBLK + e:2 * NBLK + e + 1]).then_inc(squares_done, 1)
                    act.wait_ge(squares_done, len(side))
                    act.wait_ge(sums_done, len(side))
                    for i, (b, e) in enumerate(side):
                        r0 = H - 2 if e else 0
                        act.dma_start(x1[b, :, r0:r0 + 2, :].rearrange("c r w -> c (r w)"), xa[:, 0, i * CHK:(i + 1) * CHK]).then_inc(stored[0], 16)
                    act.wait_ge(stored[0], 16 * len(side))
                    return
                act.activation(xb[:, u, :], xa[:, u, :], ACT.Square,
                               accum_out=tab["squares"][:, bass.ds(b, 1), bass.ds(t * 2 + u, 1)].rearrange("p a b -> p (a b)")).then_inc(squares_done, 1)
                act.wait_ge(squares_done, n + 1)
                act.wait_ge(sums_done, n + 1)
                act.dma_start(image(x1, b, t, u), xa[:, u, :]).then_inc(stored[u], 16)
            units(act, unit)
            if not edges:
                for u in range(2):
                    act.wait_ge(stored[u], 16 * batches * blocks)
CH_HEADS, CH_DIM = 4, 24
NCTR = 4
EM = CH_HEADS * NCTR
REG = H // 2
NREG = B * 4
NFC = 2 * C + EM


def cluster_constants():
    heads = np.zeros((C, CH_HEADS), np.float32)
    for e in range(CH_HEADS):
        heads[e * CH_DIM:(e + 1) * CH_DIM, e] = 1.0
    return {"k_heads": heads, "k_same_head": heads @ heads.T,
            "k_own_channels": np.repeat(heads.T, NCTR, axis=0).copy()}


def cluster_tables(nc, ctx):
    shapes = {"rhs": [C + 1, NREG, NFC], "value_centres": [EM, NREG, C], "eye": [128, 128], "proj": [C, C], "proj_b": [C, 1],
              "beta": [128, 1], "own_channels": [EM, C]}
    return {k: ctx.enter_context(nc.sbuf_tensor("c_" + k, s, F32)) for k, s in shapes.items()}


def cluster_setup(nc, p, tab, t):
    with ExitStack() as ctx:
        def sb(name, shape, dt=F32):
            return ctx.enter_context(nc.sbuf_tensor("cs_" + name, shape, dt))

        NBK = 16
        bsum = sb("bsum", [C, B, NBK])
        stat = sb("stat", [C, 2, B])
        avg = sb("avg", [C, 2, B])
        sq = sb("sq", [C, B])
        sd = sb("sd", [C, B])
        eps = sb("eps", [C, 1])
        scale = sb("scale", [C + 1, B])
        shift = sb("shift", [C, B])
        group = sb("group", [C, C])
        heads = sb("heads", [C, CH_HEADS])
        same = sb("same", [C, C])
        fv_t = sb("fv_t", [C, 2 * C])
        fv_b = sb("fv_b", [C + 1, 2 * C])
        f_col = sb("f_col", [C, 1])
        f_nat = sb("f_nat", [C, B, C + 1])
        alpha = sb("alpha", [C, 1])
        wfv = sb("wfv", [C + 1, B, 2 * C])
        xm = sb("xm", [C + 1, B, NBK])
        xmq = sb("xmq", [C + 1, NREG, CH_HEADS, NCTR])
        cf = sb("cf", [C, B, NBK])
        cs = sb("cs", [C, B, NBK])
        cn = sb("cn", [C, B, NBK])
        ctr = sb("ctr", [C, NREG, CH_HEADS, NCTR])
        psum = ctx.enter_context(nc.psum_tensor("cs_ps", [128, 8, 512], F32))
        loaded = ctx.enter_context(nc.semaphore("cs_loaded"))
        ones_set = ctx.enter_context(nc.semaphore("cs_ones_set"))
        dch = ctx.enter_context(nc.semaphore("cs_vector_done"))
        pch = ctx.enter_context(nc.semaphore("cs_products_done"))
        ach = ctx.enter_context(nc.semaphore("cs_roots_done"))
        stage = ctx.enter_context(nc.semaphore("cs_stage"))
        block = ctx.enter_context(nc.Block())
        loads = [(group[:], p["k_group"]), (heads[:], p["k_heads"]), (same[:], p["k_same_head"]),
                 (fv_t[:, 0:C], p["f_wt"]), (fv_t[:, C:], p["v_wt"]),
                 (fv_b[C:C + 1, 0:C], p["f_b"].rearrange("(a c) -> a c", a=1)),
                 (fv_b[C:C + 1, C:], p["v_b"].rearrange("(a c) -> a c", a=1)),
                 (f_col[:], p["f_b"].rearrange("(c a) -> c a", a=1)),
                 (f_nat[:, 0, 0:C], p["f_w"]), (f_nat[:, 1, 0:C], p["f_w"]),
                 (alpha[:], p["sim_alpha"].partition_broadcast(C)),
                 (t["beta"][:], p["sim_beta"].partition_broadcast(128)),
                 (t["eye"][:], p["k_eye"]), (t["proj"][:], p["proj_wt"]),
                 (t["proj_b"][:], p["proj_b"].rearrange("(c a) -> c a", a=1)), (t["own_channels"][:], p["k_own_channels"])]

        @block.sync
        def _(sp):
            for to, of in loads:
                sp.dma_start(to, of).then_inc(loaded, 16)

        @block.gpsimd
        def _(pool):
            pool.memset(eps[:], 1e-5).then_inc(ones_set, 1)
            pool.memset(scale[C:C + 1, :], 1.0).then_inc(ones_set, 1)
            pool.memset(xm[C:C + 1, :, :], 1.0).then_inc(ones_set, 1)

        @block.scalar
        def _(act):
            act.wait_ge(ones_set, 3)
            act.wait_ge(stage, 2)
            act.activation(sd[:], sq[:], ACT.Sqrt, bias=eps[:]).then_inc(ach, 1)
            act.wait_ge(pch, 4)
            act.activation(cs[:].rearrange("p b n -> p (b n)"), psum[0:C, 4, 0:B * NBK], ACT.Sqrt).then_inc(ach, 1)

        @block.tensor
        def _(pe):
            pe.wait_ge(loaded, 16 * len(loads))
            pe.wait_ge(stage, 1)
            pe.matmul(psum[0:C, 0, 0:2 * B], group[:], stat[:].rearrange("p a b -> p (a b)"), start=True, stop=True).then_inc(pch, 1)
            pe.wait_ge(stage, 3)
            for b in range(B):
                pe.matmul(psum[C:C + 1, 1, b * 2 * C:(b + 1) * 2 * C], shift[:, b:b + 1], fv_t[:], start=True, stop=True)
            pe.matmul(psum[0:C, 2, 0:B], fv_t[:, 0:C], shift[:], start=True, stop=True).then_inc(pch, 1)
            pe.wait_ge(stage, 4)
            for b in range(B):
                m = pe.matmul(psum[0:C, 3, b * NBK:(b + 1) * NBK], wfv[:, b, 0:C], xm[:, b, :], start=True, stop=True)
            m.then_inc(pch, 1)
            pe.wait_ge(stage, 5)
            pe.matmul(psum[0:C, 4, 0:B * NBK], same[:], cs[:].rearrange("p b n -> p (b n)"), start=True, stop=True).then_inc(pch, 1)
            pe.wait_ge(stage, 6)
            for b in range(B):
                pe.matmul(psum[0:C + 1, 5, b * 4 * EM:(b + 1) * 4 * EM], f_nat[:, b, :],
                          ctr[:, 4 * b:4 * b + 4].rearrange("p q e m -> p (q e m)"), start=True, stop=True)
            for q in range(NREG):
                m = pe.matmul(psum[0:EM, 6 + q // 4, (q % 4) * C:(q % 4 + 1) * C], xmq[:, q].rearrange("p e m -> p (e m)"),
                              wfv[:, q // 4, C:2 * C], start=True, stop=True)
            m.then_inc(pch, 1)

        @block.vector
        def _(dve):
            n = [0]

            def link(ins):
                n[0] += 1
                ins.then_inc(dch, 1)
                dve.wait_ge(dch, n[0])

            def staged():
                dve.sem_inc(stage, 1)

            rows = H // 4
            for b in range(B):
                link(dve.tensor_reduce(bsum[:, b, :].rearrange("p (i j) -> p i j", j=4),
                                       tab["row_sums"][:, b * H:(b + 1) * H, :].rearrange("p (i r) j -> p i j r", r=rows), AX.X, ALU.add))
            link(dve.tensor_reduce(stat[:, 0, :], bsum[:], AX.X, ALU.add))
            link(dve.tensor_reduce(stat[:, 1, :], tab["squares"][:], AX.X, ALU.add))
            link(dve.tensor_scalar(stat[:], stat[:], 1.0 / PIX, None, ALU.mult))
            staged()
            dve.wait_ge(pch, 1)
            link(dve.tensor_copy(avg[:].rearrange("p a b -> p (a b)"), psum[0:C, 0, 0:2 * B]))
            link(dve.tensor_tensor(sq[:], avg[:, 0, :], avg[:, 0, :], ALU.mult))
            link(dve.tensor_tensor(sq[:], avg[:, 1, :], sq[:], ALU.subtract))
            link(dve.tensor_scalar(sq[:], sq[:], 0.0, None, ALU.max))
            staged()
            dve.wait_ge(ach, 1)
            dve.wait_ge(ones_set, 3)
            link(dve.reciprocal(scale[0:C, :], sd[:]))
            link(dve.scalar_tensor_tensor(out=shift[:], in0=avg[:, 0, :], scalar=-1.0, in1=scale[0:C, :], op0=ALU.mult, op1=ALU.mult))
            staged()
            dve.wait_ge(loaded, 16 * len(loads))
            dve.wait_ge(pch, 2)
            for b in range(B):
                link(dve.tensor_scalar(wfv[0:C, b, :], fv_t[:], scale[0:C, b:b + 1], None, ALU.mult))
                link(dve.tensor_tensor(wfv[C:C + 1, b, :], psum[C:C + 1, 1, b * 2 * C:(b + 1) * 2 * C], fv_b[C:C + 1, :], ALU.add))
                link(dve.tensor_tensor(f_nat[:, b, C:C + 1], psum[0:C, 2, b:b + 1], f_col[:], ALU.add))
            link(dve.tensor_scalar(xm[0:C, :, :], bsum[:], 1.0 / (rows * rows), None, ALU.mult))
            staged()
            dve.wait_ge(pch, 3)
            link(dve.tensor_copy(cf[:].rearrange("p b n -> p (b n)"), psum[0:C, 3, 0:B * NBK]))
            link(dve.tensor_tensor(cs[:], cf[:], cf[:], ALU.mult))
            staged()
            dve.wait_ge(ach, 2)
            link(dve.tensor_scalar(cs[:], cs[:], 1e-12, None, ALU.max))
            link(dve.reciprocal(cn[:], cs[:]))
            link(dve.tensor_tensor(cn[:], cn[:], cf[:], ALU.mult))
            link(dve.tensor_scalar(cn[:], cn[:], alpha[:, 0:1], None, ALU.mult))
            for q in range(NREG):
                b, f1, f2 = q // 4, q // 2 % 2, q % 2

                def quarters(a):
                    return a[:, b, :].rearrange("p (i j) -> p i j", j=4)[:, 2 * f1:2 * f1 + 2, 2 * f2:2 * f2 + 2]
                for e in range(CH_HEADS):
                    link(dve.tensor_scalar(ctr[:, q, e, :].rearrange("p (i j) -> p i j", j=2), quarters(cn), heads[:, e:e + 1], None, ALU.mult))
                    link(dve.tensor_copy(xmq[:, q, e, :].rearrange("p (i j) -> p i j", j=2), quarters(xm)))
            staged()
            dve.wait_ge(pch, 5)
            for q in range(NREG):
                b = q // 4
                link(dve.tensor_copy(t["rhs"][:, q, 0:2 * C], wfv[:, b, :]))
                link(dve.tensor_scalar(t["rhs"][:, q, 2 * C:], psum[0:C + 1, 5, q * EM:(q + 1) * EM], scale[:, b:b + 1], None, ALU.mult))
                link(dve.tensor_copy(t["value_centres"][:, q, :], psum[0:EM, 6 + q // 4, (q % 4) * C:(q % 4 + 1) * C]))


def cluster(nc, x1, out, t, halves=B * 2):
    UROWS = 4
    NT = 8
    UT = UROWS * W
    UNITS = REG // UROWS
    SU = 4
    UPS = UNITS // SU
    TPS = UPS * NT
    VC = C + 1
    NQ = TPS * CH_HEADS
    with ExitStack() as ctx:
        def sb(name, shape, dt=F32):
            return ctx.enter_context(nc.sbuf_tensor("cl_" + name, shape, dt))

        def sem(name):
            return ctx.enter_context(nc.semaphore("cl_" + name))

        xu = sb("xu", [C + 1, 2, UT])
        sqf = sb("sqf", [128, 2, 4, C])
        val = sb("val", [128, 2, TPS, VC])
        dots = sb("dots", [128, 2, TPS, EM])
        n2 = sb("n2", [128, 2, NQ])
        nr = sb("nr", [128, NQ])
        rn = sb("rn", [128, NQ])
        sim = sb("sim", [128, NQ, NCTR])
        hit = sb("hit", [128, NQ, NCTR])
        top = sb("top", [128, NQ])
        got = sb("got", [128, NQ])
        sm = sb("sm", [128, 2, TPS, EM])
        smt = sb("smt", [128, UNITS, 128])
        zero = sb("zero", [128, 2 * VC])
        agg = sb("agg", [EM, 2, C])
        den = sb("den", [EM, 2])
        aggt = sb("aggt", [C, NT, 128])
        lhs = sb("lhs", [128, NT, C])
        ou = sb("ou", [C, 2, UT])
        psum = ctx.enter_context(nc.psum_tensor("cl_ps", [128, 8, 512], F32))
        loaded = [sem(f"loaded{i}") for i in range(2)]
        stored = [sem(f"stored{i}") for i in range(2)]
        filled, aggs = sem("filled"), sem("aggs")
        prod_done, sq_done, n2_done = sem("prod_done"), sem("sq_done"), sem("n2_done")
        out_done = sem("out_done")
        rt_done, sim_done, sg_done, sm_done, chain = sem("rt_done"), sem("sim_done"), sem("sg_done"), sem("sm_done"), sem("chain")
        tp_done, tp_out, agg_done, aggn_done, at_done, at_out, lhs_done, lhs_out = (
            sem(s) for s in ("tp_done", "tp_out", "agg_done", "aggn_done", "at_done", "at_out", "lhs_done", "lhs_out"))
        y_done, y_out = sem("y_done"), sem("y_out")
        block = ctx.enter_context(nc.Block())
        HP = 2 * UNITS
        LPH = 2 * UNITS
        LINKS = 10

        def rows(a, f, v):
            return a[bass.ds(f // 2, 1), :, bass.ds((f % 2) * REG + v * UROWS, UROWS), :].rearrange("a c r w -> (a c) (r w)")

        @block.sync
        def _(sp):
            with sp.Fori(0, halves) as f:
                for again in range(2):
                    def load(v, u):
                        sp.dma_start(xu[0:C, u, :], rows(x1, f, v)).then_inc(loaded[u], 16)

                    for u in range(2):
                        if again:
                            sp.wait_ge(prod_done, f * HP + 2 * (UNITS - 1 + u))
                        else:
                            sp.wait_ge(y_out, f * HP + 2)
                        load(u, u)
                    with sp.Fori(0, UNITS // 2 - 1) as j:
                        for u in range(2):
                            if again:
                                sp.wait_ge(y_out, f * HP + j * 4 + (2 * u + 4))
                            else:
                                sp.wait_ge(prod_done, f * HP + j * 4 + (2 * u + 2))
                            load(j * 2 + (u + 2), u)

        def wait_x(eng, f, again, j, u):
            eng.wait_ge(loaded[u], f * (16 * UNITS) + j * 16 + (again * 8 * UNITS + 16))

        @block.tensor
        def _(pe):
            pe.wait_ge(filled, 1)
            with pe.Fori(0, halves) as f:
                def products(s):
                    with pe.Fori(0, UPS // 2) as j:
                        for u in range(2):
                            wait_x(pe, f, 0, j + s * (UPS // 2), u)
                            for half in range(2):
                                n = f * HP + j * 4 + (s * 2 * UPS + 2 * u + half)
                                pe.wait_ge(out_done, n + 1)
                                for g in range(4):
                                    tile = 4 * half + g
                                    m = pe.matmul(psum[:, 2 * half + g // 2, 256 * (g % 2):256 * (g % 2) + NFC],
                                                  xu[:, u, 128 * tile:128 * tile + 128],
                                                  t["rhs"][:, bass.ds(f * 2 + tile % 2, 1), :].rearrange("p a n -> p (a n)"), start=True, stop=True)
                                m.then_inc(prod_done, 1)

                def aggregate(s):
                    b = s % 2
                    pe.wait_ge(sm_done, f * SU + (s + 1))
                    if s == 0:
                        pe.wait_ge(y_out, f * HP + 2)
                        pe.matmul(psum[0:EM, 4, 0:2 * VC], zero[:, 0:EM], zero[:], start=True, stop=False, skip_group_check=True)
                    for v in range(UPS):
                        bank = 5 + v % 2
                        n = f * UNITS + (s * UPS + v)
                        pe.wait_ge(tp_out, n + 1)
                        pe.matmul(psum[:, bank, 0:128], sm[:, b, NT * v:NT * v + NT, :].rearrange("p t e -> p (t e)"), t["eye"][:],
                                  start=True, stop=True).then_inc(tp_done, 1)
                        for g in range(NT):
                            tile = NT * v + g
                            m = pe.matmul(psum[0:EM, 4, VC * (g % 2):VC * (g % 2) + VC], sm[:, b, tile, :], val[:, b, tile, :],
                                          start=False, stop=(s == SU - 1 and tile >= TPS - 2), skip_group_check=True)
                    m.then_inc(agg_done, 1)

                for s in range(SU):
                    products(s)
                    if s:
                        aggregate(s - 1)
                aggregate(SU - 1)
                pe.wait_ge(tp_out, f * UNITS + (UNITS + 2))
                pe.wait_ge(aggn_done, f + 1)
                for i in range(2):
                    m = pe.matmul(psum[0:C, 5, i * EM:(i + 1) * EM], agg[:, i, :], t["eye"][0:EM, 0:EM], start=True, stop=True)
                m.then_inc(at_done, 1)
                pe.wait_ge(at_out, f + 1)
                for g in range(NT):
                    m = pe.matmul(psum[:, 6 + g // 4, C * (g % 4):C * (g % 4) + C], aggt[:, g, :], t["proj"][:], start=True, stop=True)
                m.then_inc(lhs_done, 1)
                with pe.Fori(0, UNITS) as v:
                    pe.wait_ge(lhs_out, f + 1)
                    for half in range(2):
                        n = f * HP + v * 2 + half
                        pe.wait_ge(y_out, n + 1)
                        for g in range(4):
                            m = pe.matmul(psum[0:C, 6 + half, 128 * g:128 * g + 128], lhs[:, 4 * half + g, :],
                                          smt[:, bass.ds(v, 1), :].rearrange("p a n -> p (a n)"), start=True, stop=True)
                        m.then_inc(y_done, 1)

        @block.scalar
        def _(act):
            act.sem_inc(out_done, 2)
            with act.Fori(0, halves) as f:
                for s in range(SU):
                    b = s % 2
                    with act.Fori(0, UPS) as j:
                        for half in range(2):
                            n = f * HP + j * 2 + (s * 2 * UPS + half)
                            act.wait_ge(prod_done, n + 1)
                            act.wait_ge(n2_done, n + 1)
                            pr = psum[:, 2 * half:2 * half + 2, :].rearrange("p a (b n) -> p (a b) n", b=2)
                            act.activation(sqf[:, half], pr[:, :, 0:C], ACT.Square).then_inc(sq_done, 1)
                            tiles = bass.ds(j * NT + 4 * half, 4)
                            act.activation(val[:, b, tiles, 0:C], pr[:, :, C:2 * C], ACT.Copy)
                            act.activation(dots[:, b, tiles, :], pr[:, :, 2 * C:NFC], ACT.Copy).then_inc(out_done, 1)
                    act.wait_ge(n2_done, f * HP + ((s + 1) * 2 * UPS + 2))
                    act.activation(nr[:], n2[:, b, :], ACT.Sqrt).then_inc(rt_done, 1)
                    act.wait_ge(sim_done, f * SU + (s + 1))
                    act.activation(sim[:], sim[:], ACT.Sigmoid, bias=t["beta"][:]).then_inc(sg_done, 1)

        @block.vector
        def _(dve):
            dve.sem_inc(n2_done, 2)
            dve.sem_inc(tp_out, 2)
            dve.sem_inc(y_out, 2)
            dve.memset(zero[:], 0.0)
            dve.memset(aggt[:], 0.0)
            dve.memset(val[:, :, :, C:VC], 1.0)
            dve.memset(xu[C:C + 1, :, :], 1.0).then_inc(filled, 1)
            with dve.Fori(0, halves) as f:
                def norms(s):
                    b = s % 2
                    with dve.Fori(0, UPS) as j:
                        for half in range(2):
                            n = f * HP + j * 2 + (s * 2 * UPS + half)
                            dve.wait_ge(sq_done, n + 1)
                            dve.tensor_reduce(n2[:, b, bass.ds(j * (NT * CH_HEADS) + half * 4 * CH_HEADS, 4 * CH_HEADS)],
                                              sqf[:, half].rearrange("p t (e c) -> p (t e) c", c=CH_DIM), AX.X, ALU.add).then_inc(n2_done, 1)

                def transposed(s):
                    for v in range(UPS):
                        dve.wait_ge(tp_done, f * UNITS + (s * UPS + v + 1))
                        dve.tensor_copy(smt[:, s * UPS + v, :], psum[:, 5 + v % 2, 0:128]).then_inc(tp_out, 1)

                def choose(s):
                    b = s % 2
                    done = [f * (SU * LINKS) + s * LINKS, 0]

                    def link(ins):
                        done[1] += 1
                        ins.then_inc(chain, 1)
                        dve.wait_ge(chain, done[0] + done[1])

                    dve.wait_ge(rt_done, f * SU + (s + 1))
                    link(dve.tensor_scalar(nr[:], nr[:], 1e-12, None, ALU.max))
                    link(dve.reciprocal(rn[:], nr[:]))
                    dve.wait_ge(out_done, f * HP + ((s + 1) * 2 * UPS + 2))
                    dve.tensor_tensor(sim[:], dots[:, b].rearrange("p t (e m) -> p (t e) m", m=NCTR),
                                      rn[:].unsqueeze(2).to_broadcast([128, NQ, NCTR]), ALU.mult).then_inc(sim_done, 1)
                    dve.wait_ge(sg_done, f * SU + (s + 1))
                    link(dve.tensor_reduce(top[:], sim[:], AX.X, ALU.max))
                    link(dve.tensor_tensor(hit[:], sim[:], top[:].unsqueeze(2).to_broadcast([128, NQ, NCTR]), ALU.is_equal))
                    link(dve.tensor_tensor(hit[:, :, 1], hit[:, :, 1], hit[:, :, 0], ALU.is_gt))
                    link(dve.tensor_tensor(got[:], hit[:, :, 1], hit[:, :, 0], ALU.max))
                    link(dve.tensor_tensor(hit[:, :, 2], hit[:, :, 2], got[:], ALU.is_gt))
                    link(dve.tensor_tensor(got[:], hit[:, :, 2], got[:], ALU.max))
                    link(dve.tensor_tensor(hit[:, :, 3], hit[:, :, 3], got[:], ALU.is_gt))
                    link(dve.tensor_tensor(sm[:, b].rearrange("p t (e m) -> p (t e) m", m=NCTR), sim[:], hit[:], ALU.mult))
                    dve.sem_inc(sm_done, 1)
                    assert done[1] == LINKS

                for s in range(SU):
                    norms(s)
                    if s:
                        transposed(s - 1)
                    choose(s)
                transposed(SU - 1)
                dve.wait_ge(agg_done, f * SU + SU)
                sums = psum[0:EM, 4, 0:2 * VC].rearrange("p (i n) -> p i n", n=VC)
                dve.tensor_scalar(den[:], sums[:, :, C], 1.0, None, ALU.add).then_inc(aggs, 1)
                dve.tensor_tensor(agg[:], sums[:, :, 0:C], t["value_centres"][:, bass.ds(f * 2, 2), :], ALU.add).then_inc(aggs, 1)
                dve.wait_ge(aggs, f * 4 + 2)
                dve.reciprocal(den[:], den[:]).then_inc(aggs, 1)
                dve.wait_ge(aggs, f * 4 + 3)
                dve.tensor_tensor(agg[:], agg[:], den[:].unsqueeze(2).to_broadcast([EM, 2, C]), ALU.mult).then_inc(aggs, 1)
                dve.wait_ge(aggs, f * 4 + 4)
                dve.tensor_tensor(agg[:], agg[:], t["own_channels"][:].unsqueeze(1).to_broadcast([EM, 2, C]), ALU.mult).then_inc(aggn_done, 1)
                dve.wait_ge(at_done, f + 1)
                for g in range(NT):
                    i = dve.tensor_copy(aggt[:, g, EM * g:EM * g + EM], psum[0:C, 5, (g % 2) * EM:(g % 2 + 1) * EM])
                i.then_inc(at_out, 1)
                dve.wait_ge(lhs_done, f + 1)
                for i in range(2):
                    ins = dve.tensor_copy(lhs[:, 4 * i:4 * i + 4, :], psum[:, 6 + i, 0:4 * C].rearrange("p (g n) -> p g n", n=C))
                ins.then_inc(lhs_out, 1)
                with dve.Fori(0, UNITS // 2) as j:
                    for u in range(2):
                        wait_x(dve, f, 1, j, u)
                        dve.wait_ge(stored[u], f * (8 * UNITS) + j * 16)
                        for half in range(2):
                            dve.wait_ge(y_done, f * HP + j * 4 + (2 * u + half + 1))
                            at = slice(512 * half, 512 * half + 512)
                            dve.scalar_tensor_tensor(out=ou[:, u, at], in0=psum[0:C, 6 + half, :], scalar=t["proj_b"][:, 0:1],
                                                           in1=xu[0:C, u, at], op0=ALU.add, op1=ALU.add).then_inc(y_out, 1)

        @block.gpsimd
        def _(pool):
            with pool.Fori(0, halves) as f:
                with pool.Fori(0, UNITS // 2) as j:
                    for u in range(2):
                        pool.wait_ge(y_out, f * HP + j * 4 + (2 * u + 4))
                        pool.dma_start(rows(out, f, j * 2 + u), ou[:, u, :]).then_inc(stored[u], 16)
            for u in range(2):
                pool.wait_ge(stored[u], 8 * UNITS * halves)


_NAMES = {"norm1_w": "L0_conv_norm1_w", "norm1_b": "L0_conv_norm1_b", "wq": "L0_conv_wq", "wk": "L0_conv_wk", "wv": "L0_conv_wv",
          "wproj": "L0_conv_wproj", "norm2_w": "L0_conv_norm2_w", "norm2_b": "L0_conv_norm2_b", "fc1_w": "L0_conv_fc1_w",
          "fc1_b": "L0_conv_fc1_b", "dw_w": "L0_conv_dw_w", "dw_b": "L0_conv_dw_b", "fc2_w": "L0_conv_fc2_w", "fc2_b": "L0_conv_fc2_b",
          "f_w": "L1_conv_f_w", "f_b": "L1_conv_f_b", "v_b": "L1_conv_v_b", "proj_b": "L1_conv_proj_b",
          "sim_alpha": "L1_conv_sim_alpha", "sim_beta": "L1_conv_sim_beta"}
_TRANSPOSED = {"f_wt": "L1_conv_f_w", "v_wt": "L1_conv_v_w", "proj_wt": "L1_conv_proj_w"}


def program(nc, p, out):
    x = p["x"]
    x2 = nc.dram_tensor("x2", (B, C, H, W), F32).ap()
    x1 = nc.dram_tensor("x1", (B, C, H, W), F32).ap()
    ydr = nc.dram_tensor("y_mlp", (MLP, H, B, W), F32).ap()
    sdr = nc.dram_tensor("s_mlp", (NBLK, MLP, BLK, B, W), F32).ap()
    with ExitStack() as ctx:
        t = attention_tables(nc, ctx)
        group_norm_statistics(nc, x, t)
        attention_setup(nc, p, t)
        attention(nc, x, x2, t)
    fc1(nc, p, x2, ydr)
    conv(nc, p, ydr, sdr)
    with ExitStack() as ctx:
        tab = {"row_sums": ctx.enter_context(nc.sbuf_tensor("row_sums", [C, B * H, 4], F32)),
               "squares": ctx.enter_context(nc.sbuf_tensor("squares", [C, B, 2 * NBLK + 2], F32))}
        t = cluster_tables(nc, ctx)
        fc2(nc, p, x, x2, sdr, x1, tab, True)
        fc2(nc, p, x, x2, sdr, x1, tab, False)
        cluster_setup(nc, p, tab, t)
        cluster(nc, x1, out, t)


def kernel(**inputs):
    import numpy as _np
    import concourse.bacc as _bacc
    from concourse import mybir as _mybir
    from concourse.bass_utils import run_bass_kernel_spmd as _run

    nc = _bacc.Bacc("TRN2", target_bir_lowering=False, num_devices=1)
    arrays = {"x": inputs["x"]}
    arrays.update({name: inputs[of] for name, of in _NAMES.items()})
    arrays.update({name: _np.asarray(inputs[of]).T for name, of in _TRANSPOSED.items()})
    arrays.update(constants())
    arrays.update(conv_constants())
    arrays.update(cluster_constants())
    p, feeds = {}, {}
    for name, a in arrays.items():
        a = _np.ascontiguousarray(a)
        feeds[f"in_{name}"] = a
        p[name] = nc.dram_tensor(f"in_{name}", a.shape, _mybir.dt.from_np(a.dtype), kind="ExternalInput").ap()
    out = nc.dram_tensor("out", (B, C, H, W), F32, kind="ExternalOutput").ap()
    program(nc, p, out)
    r = _run(nc, [feeds], core_ids=[0])
    return r.results[0]["out"]
```

```python
from contextlib import ExitStack

import numpy as np

import concourse.bass as bass
from concourse import mybir

F32 = mybir.dt.float32
BF16 = mybir.dt.bfloat16
ALU = mybir.AluOpType
ACT = mybir.ActivationFunctionType
AX = mybir.AxisListType

B, C, H, W = 2, 96, 256, 256
PS, STEP = 16, 14
NWIN = 19
LAST = H - PS
HEADS, DQ, DV = 4, 16, 24
TOK = PS * PS
GROUP = 3
MLP = 192
PIX = H * W
BASE = 64


def start_semaphores(nc, semaphores):
    with nc.Block() as block:
        @block.gpsimd
        def _(pool):
            for s in semaphores:
                pool.sem_inc(s, BASE)


def constants():
    eye = np.eye(128, dtype=np.float32)
    centre = np.eye(C, dtype=np.float32) - np.float32(1.0 / C)
    group = np.zeros((C, C), np.float32)
    for g in range(C // GROUP):
        group[g * GROUP:(g + 1) * GROUP, g * GROUP:(g + 1) * GROUP] = 1.0 / GROUP
    head_rows = np.zeros((128, HEADS), np.float32)
    for h in range(HEADS):
        head_rows[32 * h:32 * h + 32, h] = 1.0
    one_rows = np.zeros((128, 1), np.float32)
    one_rows[DQ::32] = 1.0
    first_rows = np.full((C, NWIN), 0.5, np.float32)
    first_rows[:, 0] = 1.0
    return {"k_eye": eye, "k_centre": centre, "k_group": group, "k_head_rows": head_rows,
            "k_one_rows": one_rows, "k_first_rows": first_rows, "k_first_rows_inverse": 1.0 / first_rows}


def group_norm_statistics(nc, x, t):
    CH, PART, FM = 8192, 8, 512
    with ExitStack() as ctx:
        xin = ctx.enter_context(nc.sbuf_tensor("gn_xin", [C, 2, CH], F32))
        stats = ctx.enter_context(nc.sbuf_tensor("gn_stats", [C, B * PIX // FM, 6], F32))
        loaded = [ctx.enter_context(nc.semaphore(f"gn_loaded{i}")) for i in range(2)]
        read = ctx.enter_context(nc.semaphore("gn_read"))
        aggregated = ctx.enter_context(nc.semaphore("gn_aggregated"))
        block = ctx.enter_context(nc.Block())
        rows = H // PART
        steps = B * PART

        def part(m):
            b, q = m // PART, m % PART
            return x[bass.ds(b, 1), :, bass.ds(q * rows, rows), :].rearrange("a c r w -> (a c) (r w)")

        @block.sync
        def _(sp):
            for i in range(2):
                sp.dma_start(xin[:, i, :], part(i)).then_inc(loaded[i], 16)
            with sp.Fori(0, steps // 2 - 1) as s:
                for i in range(2):
                    sp.wait_ge(read, 2 * s + i + 1)
                    sp.dma_start(xin[:, i, :], part(2 * s + (i + 2))).then_inc(loaded[i], 16)

        @block.vector
        def _(dve):
            per = CH // FM
            with dve.Fori(0, steps // 2) as s:
                for i in range(2):
                    dve.wait_ge(loaded[i], 16 * s + 16)
                    for k in range(per):
                        last = dve.bn_stats(stats[:, bass.ds((2 * s + i) * per + k, 1), :].rearrange("p a b -> p (a b)"), xin[:, i, k * FM:(k + 1) * FM])
                    last.then_inc(read, 1)
            dve.wait_ge(read, steps)
            for b in range(B):
                n = PIX // FM
                dve.bn_aggr(t["mean_var"][:, b, :], stats[:, b * n:(b + 1) * n, :]).then_inc(aggregated, 1)
            dve.wait_ge(aggregated, B)


def attention_setup(nc, p, t):
    with ExitStack() as ctx:
        def sb(name, shape, dt=F32):
            return ctx.enter_context(nc.sbuf_tensor("as_" + name, shape, dt))
        m2 = sb("m2", [C, 2, B])
        avg = sb("avg", [C, 2, B])
        sq = sb("sq", [C, B])
        sd = sb("sd", [C, B])
        group = sb("group", [C, C])
        n1 = sb("n1", [C, 2])
        one_rows = sb("one_rows", [128, 1])
        bv = sb("bv", [C, 1])
        eps = sb("eps", [C, 1])
        ps = ctx.enter_context(nc.psum_tensor("as_ps", [128, 4, 512], F32))
        loaded = ctx.enter_context(nc.semaphore("as_loaded"))
        dch = ctx.enter_context(nc.semaphore("as_vector_done"))
        pch = ctx.enter_context(nc.semaphore("as_products_done"))
        ach = ctx.enter_context(nc.semaphore("as_roots_done"))
        cleared = ctx.enter_context(nc.semaphore("as_cleared"))
        block = ctx.enter_context(nc.Block())
        nload = 14

        @block.gpsimd
        def _(pool):
            pool.memset(t["wqk"][:], 0.0).then_inc(cleared, 1)
            pool.memset(t["mz"][:], 0.0).then_inc(cleared, 1)
            pool.memset(t["vaug"][:], 1.0).then_inc(cleared, 1)
            pool.memset(t["acc"][:], 0.0).then_inc(cleared, 1)
            pool.memset(t["eps5"][:], 1e-5).then_inc(cleared, 1)
            pool.memset(eps[:], 1e-5).then_inc(cleared, 1)
            pool.memset(t["ones"][:], 1.0 / C).then_inc(cleared, 1)
            pool.memset(t["zero"][:], 0.0).then_inc(cleared, 1)
            pool.memset(t["one"][:], 1.0).then_inc(cleared, 1)

        @block.sync
        def _(sp):
            sp.wait_ge(cleared, 9)
            for i, name in enumerate(("wq", "wk")):
                for h in range(HEADS):
                    sp.dma_start(t["wqk"][:, i, 32 * h:32 * h + DQ], p[name][:, h * DQ:(h + 1) * DQ]).then_inc(loaded, 16)
            sp.dma_start(t["wv"][:], p["wv"]).then_inc(loaded, 16)
            sp.dma_start(t["wproj"][:], p["wproj"]).then_inc(loaded, 16)
            sp.dma_start(n1[:, 0:1], p["norm1_w"].rearrange("(c a) -> c a", a=1)).then_inc(loaded, 16)
            sp.dma_start(n1[:, 1:2], p["norm1_b"].rearrange("(c a) -> c a", a=1)).then_inc(loaded, 16)
            sp.dma_start(group[:], p["k_group"]).then_inc(loaded, 16)
            sp.dma_start(one_rows[:], p["k_one_rows"]).then_inc(loaded, 16)
            for k in ("eye", "centre", "head_rows", "first_rows", "first_rows_inverse"):
                sp.dma_start(t[k][:], p["k_" + k]).then_inc(loaded, 16)

        nload += 5

        @block.scalar
        def _(act):
            act.wait_ge(dch, 4)
            act.activation(sd[:], sq[:], ACT.Sqrt, bias=eps[:]).then_inc(ach, 1)

        @block.tensor
        def _(pe):
            pe.wait_ge(loaded, 16 * nload)
            pe.wait_ge(dch, 2)
            pe.matmul(ps[0:C, 0, 0:2 * B], group[:], m2[:].rearrange("p a b -> p (a b)"), start=True, stop=True).then_inc(pch, 1)
            pe.matmul(ps[:, 1, 0:1], t["wqk"][:, 0, :], n1[:, 1:2], start=True, stop=True)
            pe.matmul(ps[:, 1, 1:2], t["wqk"][:, 1, :], n1[:, 1:2], start=True, stop=True)
            pe.matmul(ps[0:C, 1, 2:3], t["wv"][:], n1[:, 1:2], start=True, stop=True).then_inc(pch, 1)
            pe.wait_ge(dch, 6)
            pe.matmul(ps[0:C, 2, 0:1], t["wproj"][:], bv[:], start=True, stop=True)
            pe.wait_ge(dch, 9)
            pe.matmul(ps[0:C, 3, 0:B], t["centre"][:], t["gn_shift"][:], start=True, stop=True).then_inc(pch, 1)

        @block.vector
        def _(dve):
            n = [0]

            def link(ins):
                n[0] += 1
                ins.then_inc(dch, 1)
                dve.wait_ge(dch, n[0])

            mv = t["mean_var"]
            dve.wait_ge(loaded, 16 * nload)
            link(dve.tensor_tensor(m2[:, 1, :], mv[:, :, 0], mv[:, :, 0], ALU.mult))
            dve.tensor_copy(m2[:, 0, :], mv[:, :, 0])
            link(dve.tensor_tensor(m2[:, 1, :], m2[:, 1, :], mv[:, :, 1], ALU.add))
            dve.wait_ge(pch, 1)
            dve.tensor_copy(avg[:].rearrange("p a b -> p (a b)"), ps[0:C, 0, 0:2 * B]).then_inc(dch, 1)
            n[0] += 1
            dve.wait_ge(dch, n[0])
            dve.tensor_tensor(sq[:], avg[:, 0, :], avg[:, 0, :], ALU.mult).then_inc(ach, 1)
            dve.wait_ge(ach, 1)
            link(dve.tensor_tensor(sq[:], avg[:, 1, :], sq[:], ALU.subtract))
            dve.wait_ge(pch, 2)
            link(dve.tensor_scalar(t["qk_bias"][:, 0:1], ps[:, 1, 0:1], 0.25, None, ALU.mult))
            link(dve.tensor_copy(bv[:], ps[0:C, 1, 2:3]))
            link(dve.tensor_tensor(t["qk_bias"][:, 1:2], ps[:, 1, 1:2], one_rows[:], ALU.add))
            dve.wait_ge(ach, 2)
            link(dve.reciprocal(t["gn_scale"][:], sd[:]))
            link(dve.scalar_tensor_tensor(out=t["gn_shift"][:], in0=avg[:, 0, :], scalar=-1.0, in1=t["gn_scale"][:], op0=ALU.mult, op1=ALU.mult))
            dve.wait_ge(pch, 3)
            link(dve.tensor_copy(t["cen_shift"][:], ps[0:C, 3, 0:B]))
            for b in range(B):
                link(dve.tensor_tensor(t["out_shift"][:, b:b + 1], ps[0:C, 2, 0:1], t["gn_shift"][:, b:b + 1], ALU.add))
                link(dve.tensor_scalar(t["cen_w"][:, b, :], t["centre"][:], t["gn_scale"][:, b:b + 1], None, ALU.mult))
            link(dve.tensor_scalar(t["wqk"][:, 0, :], t["wqk"][:, 0, :], n1[:, 0:1], 0.25, ALU.mult, ALU.mult))
            link(dve.tensor_scalar(t["wqk"][:, 1, :], t["wqk"][:, 1, :], n1[:, 0:1], None, ALU.mult))
            link(dve.tensor_scalar(t["wv"][:], t["wv"][:], n1[:, 0:1], None, ALU.mult))
            link(dve.tensor_scalar(t["neg_eye"][:], t["eye"][:], -1.0, None, ALU.mult))


def layer_norm(nc, x, ydr, t, groups=H // 16):
    CK = 512
    NTOK = 16 * W
    NCK = NTOK // CK
    NT = NTOK // 128
    with ExitStack() as ctx:
        sems = []

        def sb(name, shape, dt=F32):
            return ctx.enter_context(nc.sbuf_tensor("ln_" + name, shape, dt))

        def sem(name):
            sems.append(ctx.enter_context(nc.semaphore("ln_" + name)))
            return sems[-1]

        xin = sb("xin", [C, 2, NTOK])
        z = sb("z", [C, 2, NTOK])
        sq = sb("sq", [C, 2, CK])
        sd = sb("sd", [128, NT])
        rs = sb("rs", [128, NT])
        psum = ctx.enter_context(nc.psum_tensor("ln_ps", [128, 8, 512], F32))
        x_loaded = [ctx.enter_context(nc.semaphore(f"ln_x_loaded{i}")) for i in range(2)]
        stored = [[ctx.enter_context(nc.semaphore(f"ln_stored{i}_{half}")) for half in range(2)] for i in range(2)]
        cen_done, cs_done, sq_done, var_done, sd_done, rs_done, bc_done, z_done = (
            sem(s) for s in ("cen_done", "cs_done", "sq_done", "var_done", "sd_done", "rs_done", "bc_done", "z_done"))
        start_semaphores(nc, sems)
        block = ctx.enter_context(nc.Block())

        def rows_of(a, b, r):
            return a[b, :, bass.ds(r * 16, 16), :].rearrange("c r w -> c (r w)")

        def steps(eng, step):
            for b in range(B):
                k0 = b * groups
                step(0, b, 0, k0, True, b > 0)
                with eng.Fori(0, groups // 2 - 1) as j:
                    step(1, b, 2 * j + 1, 2 * j + (k0 + 1), True, True)
                    step(0, b, 2 * j + 2, 2 * j + (k0 + 2), True, True)
                step(1, b, groups - 1, k0 + groups - 1, True, True)
            step(0, B, 0, B * groups, False, True)

        @block.sync
        def _(sp):
            def step(u, b, r, k, stats, products):
                if stats:
                    sp.wait_ge(cen_done, BASE + (k - 1) * NCK)
                    sp.dma_start(xin[:, u, :], rows_of(x, b, r)).then_inc(x_loaded[u], 16)
            steps(sp, step)

        @block.gpsimd
        def _(pool):
            def step(u, b, r, k, stats, products):
                if stats:
                    for half in range(2):
                        pool.wait_ge(z_done, BASE + k * NCK + (half + 1) * (NCK // 2))
                        pool.dma_start(ydr[b, :, bass.ds(r * 16 + half * 8, 8), :].rearrange("c r w -> c (r w)"),
                                       z[:, u, half * (NTOK // 2):(half + 1) * (NTOK // 2)]).then_inc(stored[u][half], 16)
            steps(pool, step)
            for i in range(2):
                for half in range(2):
                    pool.wait_ge(stored[i][half], 8 * B * groups)

        @block.tensor
        def _(pe):
            def step(u, b, r, k, stats, products):
                base, was = k * NCK, (k - 1) * NCK

                def variance(c):
                    pe.wait_ge(sq_done, BASE + base + (c + 1))
                    if c == 0:
                        pe.wait_ge(sd_done, BASE + k)
                    for s in range(CK // 128):
                        m = pe.matmul(psum[:, 3, 4 * c + s:4 * c + s + 1], sq[:, c % 2, 128 * s:128 * s + 128], t["ones"][:],
                                      start=True, stop=True)
                    m.then_inc(var_done, 1)

                if stats:
                    pe.wait_ge(x_loaded[u], 8 * (k - u) + 16)
                for c in range(NCK):
                    if stats:
                        if c >= 3:
                            pe.wait_ge(cs_done, BASE + base + (c - 2))
                        pe.matmul(psum[0:C, c % 3, :], t["cen_w"][:, b, :], xin[:, u, c * CK:(c + 1) * CK], start=True, stop=True).then_inc(cen_done, 1)
                        if c >= 1:
                            variance(c - 1)
                    if products:
                        if c == 0:
                            pe.wait_ge(rs_done, BASE + k)
                        pe.wait_ge(z_done, BASE + was + (c - 3))
                        for s in range(CK // 128):
                            m = pe.matmul(psum[0:C, 4 + c % 4, 128 * s:128 * s + 128],
                                          rs[:, 4 * c + s:4 * c + s + 1].to_broadcast([128, C]), t["eye"][:], start=True, stop=True)
                        m.then_inc(bc_done, 1)
                if stats:
                    variance(NCK - 1)
                    pe.wait_ge(cs_done, BASE + base + NCK)
            steps(pe, step)

        @block.scalar
        def _(act):
            def step(u, b, r, k, stats, products):
                if not stats:
                    return
                base = k * NCK
                for c in range(NCK):
                    if c % (NCK // 2) == 0:
                        act.wait_ge(stored[u][c // (NCK // 2)], 8 * (k - u))
                    act.wait_ge(cen_done, BASE + base + (c + 1))
                    act.activation(z[:, u, c * CK:(c + 1) * CK], psum[0:C, c % 3, :], ACT.Identity, bias=t["cen_shift"][:, b:b + 1]).then_inc(cs_done, 1)
                act.wait_ge(var_done, BASE + base + NCK)
                act.activation(sd[:], psum[:, 3, 0:NT], ACT.Sqrt, bias=t["eps5"][:]).then_inc(sd_done, 1)
            steps(act, step)

        @block.vector
        def _(dve):
            def step(u, b, r, k, stats, products):
                base, was = k * NCK, (k - 1) * NCK
                for c in range(NCK):
                    if stats:
                        dve.wait_ge(cs_done, BASE + base + (c + 1))
                        dve.wait_ge(var_done, BASE + base + (c - 1))
                        zc = z[:, u, c * CK:(c + 1) * CK]
                        dve.tensor_tensor(sq[:, c % 2, :], zc, zc, ALU.mult).then_inc(sq_done, 1)
                    if products:
                        dve.wait_ge(bc_done, BASE + was + (c + 1))
                        zc = z[:, 1 - u, c * CK:(c + 1) * CK]
                        dve.tensor_tensor(zc, psum[0:C, 4 + c % 4, :], zc, ALU.mult).then_inc(z_done, 1)
                if stats:
                    dve.wait_ge(sd_done, BASE + k + 1)
                    dve.wait_ge(bc_done, BASE + base)
                    dve.reciprocal(rs[:], sd[:]).then_inc(rs_done, 1)
            steps(dve, step)


def attention(nc, x, yln, x2, t, batches=B, bands=NWIN - 1):
    VW = DV + 1
    PIECES = 8
    with ExitStack() as ctx:
        def sb(name, shape, dt=F32):
            return ctx.enter_context(nc.sbuf_tensor("at_" + name, shape, dt))

        sems = []

        def sem(name):
            sems.append(ctx.enter_context(nc.semaphore("at_" + name)))
            return sems[-1]

        xin = sb("xin", [C, PS * W])
        xg = sb("xg", [C, PS * W])
        y = sb("y", [C, PS * W])
        out = sb("out", [C, PS * W])
        win = sb("win", [C, 2, TOK])
        q = sb("q", [128, 2, TOK])
        k = sb("k", [128, 2, TOK])
        kz = sb("kz", [128, 2, HEADS, TOK])
        qaug = sb("qaug", [128, TOK])
        E = sb("E", [128, 2, HEADS, 2 * TOK])
        rden = sb("rden", [128, 8])
        on = sb("on", [128, 2, C])
        ot = sb("ot", [C, TOK])
        scale = sb("scale", [C, 1])
        shift = sb("shift", [C, 1])
        psum = ctx.enter_context(nc.psum_tensor("at_ps", [128, 8, 512], F32))
        acc, vaug, mz = t["acc"], t["vaug"], t["mz"]
        qk_ps = psum[:, 4, :]
        vt_ps = psum[:, 5, :]
        pv_ps = psum[:, 6, :]
        pr_ps = psum[:, 7, :]
        qb = q[:].bitcast(BF16).rearrange("p b (n two) -> p b n two", two=2)[:, :, :, 1]
        kb = kz[:].bitcast(BF16).rearrange("p b h (n two) -> p b h n two", two=2)[:, :, :, :, 1]

        x_loaded, y_loaded, stored = (ctx.enter_context(nc.semaphore("at_" + name)) for name in ("x_loaded", "y_loaded", "stored"))
        batch_set, xg_parts, xg_scaled = sem("batch_set"), sem("xg_parts"), sem("xg_scaled")
        win_ready, kz_ready = sem("win_ready"), sem("kz_ready")
        qk_done, v_done, s1_done, t_done, s2_done, pv_done, ot_done, proj_done = (
            sem(s) for s in ("qk_done", "v_done", "s1_done", "t_done", "s2_done", "pv_done", "ot_done", "proj_done"))
        qk_out, exp_done, ot_out = sem("qk_out"), sem("exp_done"), sem("ot_out")
        v_out, max_done, qaug_done, rden_done, norm_done, added = (
            sem(s) for s in ("v_out", "max_done", "qaug_done", "rden_done", "norm_done", "added"))
        summed, carried, acc_ready, out_rows, out_done = (
            sem(s) for s in ("summed", "carried", "acc_ready", "out_rows", "out_done"))
        start_semaphores(nc, sems)
        block = ctx.enter_context(nc.Block())

        def each_band(eng, body, start=None):
            with eng.Fori(0, batches) as b:
                if start is not None:
                    start(b)
                with eng.Fori(0, bands) as r:
                    body(b * (bands + 1) + r, r, False, b)
                body(b * (bands + 1) + bands, bands, True, b)

        def each_step(eng, n, step):
            base = n * NWIN
            step(1, base + 1, 1)
            with eng.Fori(0, 7) as j:
                for u in range(2):
                    step(2 + u, base + 2 * j + (2 + u), 2 * j + (2 + u))
            for i in range(16, NWIN + 2):
                step(i, base + i, i)

        def newest(i, Wd):
            return (0, Wd - 1) if i == NWIN + 1 else (i, Wd)

        def column(w):
            return LAST if isinstance(w, int) and w == NWIN - 1 else w * STEP

        def shared_columns(a):
            rows = a[:].rearrange("p (r c) -> p r c", c=W)
            return (rows[:, :, STEP:STEP * (NWIN - 1)].rearrange("p r (g s) -> p r g s", s=STEP)[:, :, :, 0:PS - STEP],
                    rows[:, :, LAST:LAST + STEP])

        def window(a, w):
            return a[:].rearrange("p (r c) -> p r c", c=W)[:, :, bass.ds(column(w), PS)]

        @block.sync
        def _(sp):
            def body(n, r, last, b):
                row = LAST if last else r * STEP
                sp.wait_ge(win_ready, BASE + n * NWIN)
                sp.dma_start(y[:], yln[bass.ds(b, 1), :, bass.ds(row, PS), :].rearrange("a c r w -> (a c) (r w)")).then_inc(y_loaded, 16)
                sp.wait_ge(xg_parts, BASE + PIECES * n)
                sp.dma_start(xin[:], x[bass.ds(b, 1), :, bass.ds(row, PS), :].rearrange("a c r w -> (a c) (r w)")).then_inc(x_loaded, 16)
            each_band(sp, body)
            sp.wait_ge(win_ready, BASE + batches * (bands + 1) * NWIN)
            sp.dma_start(y[:], yln[0, :, 0:PS, :].rearrange("c r w -> c (r w)")).then_inc(y_loaded, 16)

        @block.gpsimd
        def _(pool):
            def copy(to, of):
                one = t["one"][:]
                for _ in of.shape[2:]:
                    one = one.unsqueeze(1)
                return pool.tensor_tensor(to, of, one.to_broadcast(list(of.shape)), ALU.mult)

            def gather(i, Wd, w, before):
                pool.wait_ge(v_done, BASE + before)
                copy(win[:, i % 2, :].rearrange("p (r c) -> p r c", c=PS), window(y, w)).then_inc(win_ready, 1)

            def mask(i, Wd, before):
                pool.wait_ge(qk_out, BASE + Wd + 1)
                for h in range(HEADS):
                    pool.wait_ge(s2_done, BASE + HEADS * before + (h + 1))
                    pool.tensor_tensor(kz[:, i % 2, h, :], k[:, i % 2, :], t["head_rows"][:, h:h + 1].to_broadcast([128, TOK]),
                                       ALU.mult).then_inc(kz_ready, 1)

            def prepare(i, Wd, w):
                if i < NWIN - 2:
                    gather(i + 2, Wd + 2, w + 2, Wd + 1)
                if i < NWIN - 1:
                    mask(i + 1, Wd + 1, Wd - 1)

            def body(n, r, last, b):
                def step(i, Wd, w):
                    if i == NWIN:
                        gather(1, Wd + 1, 1, Wd)
                        mask(0, Wd, Wd - 1)
                    else:
                        i0, W0 = newest(i, Wd)
                        prepare(i0, W0, 0 if i0 == 0 else w)
                    if i == NWIN - 1:
                        pool.wait_ge(y_loaded, 16 * n + 32)
                        gather(0, Wd + 1, 0, Wd + 1)
                each_step(pool, n, step)

            pool.wait_ge(y_loaded, 16)
            gather(0, 0, 0, 0)
            gather(1, 1, 1, 0)
            mask(0, 0, -1)
            prepare(0, 0, 0)
            each_band(pool, body)

        @block.scalar
        def _(act):
            def queries_and_keys(i, Wd, before):
                act.wait_ge(qk_done, BASE + Wd + 1)
                act.wait_ge(qaug_done, BASE + before)
                act.wait_ge(kz_ready, BASE + HEADS * before)
                act.activation(q[:, i % 2, :], qk_ps[:, 0:TOK], ACT.Identity, bias=t["qk_bias"][:, 0:1])
                act.activation(k[:, i % 2, :], qk_ps[:, TOK:], ACT.Identity, bias=t["qk_bias"][:, 1:2]).then_inc(qk_out, 1)

            def copy(to, of):
                return act.activation(to, of, ACT.Copy)

            def clear(to):
                return copy(to, t["zero"][:].to_broadcast([C, to.shape[1]]))

            def body(n, r, last, b):
                chain = b * (bands + 3) + r

                def sums():
                    if last:
                        act.wait_ge(stored, 16 * n)
                        copy(out[:, 0:STEP * W], acc[:, 2 * W:]).then_inc(carried, 1)
                        act.wait_ge(carried, BASE + chain + 1)
                        copy(acc[:, 0:STEP * W], out[:, 0:STEP * W]).then_inc(carried, 1)
                        act.wait_ge(carried, BASE + chain + 2)
                        clear(acc[:, STEP * W:]).then_inc(acc_ready, 1)
                    else:
                        copy(acc[:, 0:2 * W], acc[:, STEP * W:]).then_inc(carried, 1)
                        act.wait_ge(carried, BASE + chain + 1)
                        clear(acc[:, 2 * W:]).then_inc(acc_ready, 1)

                def step(i, Wd, w):
                    W1, W2 = Wd - 1, Wd - 2

                    def exponential(h):
                        if i <= NWIN:
                            if h == 0:
                                act.wait_ge(pv_done, BASE + (W1 if i == 1 else W1 - 1))
                            act.wait_ge(s2_done, BASE + HEADS * W1 + (h + 1))
                            act.activation(E[:, (i - 1) % 2, h, :], psum[:, 2 + h % 2, :], ACT.Exp).then_inc(exp_done, 1)

                    exponential(0)
                    if i >= 2:
                        act.wait_ge(ot_done, BASE + W2 + 1)
                        act.wait_ge(proj_done, BASE + W2)
                        act.activation(ot[:], pr_ps[0:C, 0:TOK], ACT.Copy).then_inc(ot_out, 1)
                    exponential(1)
                    i0, W0 = newest(i, Wd)
                    if i == NWIN:
                        queries_and_keys(0, Wd, Wd)
                    elif i0 < NWIN - 1:
                        queries_and_keys(i0 + 1, W0 + 1, W0)
                    exponential(2)
                    exponential(3)
                    if i == 1:
                        sums()
                    if i >= 2 and i % 2 == 0 and i < NWIN - 1 and not isinstance(w, int):
                        group_norm((w - 2) * W)
                    if i == NWIN - 3:
                        group_norm((PIECES - 1) * 2 * W)

                def group_norm(first):
                    act.activation(xg[:, bass.ds(first, 2 * W)], xin[:, bass.ds(first, 2 * W)], ACT.Identity,
                                   bias=shift[:], scale=scale[:]).then_inc(xg_parts, 1)

                act.wait_ge(summed, BASE + 2 * n)
                act.wait_ge(batch_set, BASE + 2 * b + 2)
                act.wait_ge(x_loaded, 16 * n + 16)
                each_step(act, n, step)
                act.wait_ge(out_rows, BASE + n + 1)
                for part in shared_columns(out):
                    act.activation(part, part, ACT.Copy, scale=0.5).then_inc(out_done, 1)
                act.wait_ge(out_done, BASE + 2 * n + 2)
                rows = PS if last else STEP
                row = LAST if last else r * STEP
                act.dma_start(x2[bass.ds(b, 1), :, bass.ds(row, rows), :].rearrange("a c r w -> (a c) (r w)"),
                              out[:, 0:rows * W]).then_inc(stored, 16)
                if last:
                    clear(acc[:, STEP * W:]).then_inc(carried, 1)
                    act.wait_ge(carried, BASE + chain + 3)

            queries_and_keys(0, 0, 0)
            queries_and_keys(1, 1, 0)
            each_band(act, body)
            act.wait_ge(stored, 16 * batches * (bands + 1))

        @block.tensor
        def _(pe):
            def queries_and_keys(i, Wd):
                pe.wait_ge(win_ready, BASE + Wd + 1)
                pe.wait_ge(qk_out, BASE + Wd)
                for z in range(2):
                    m = pe.matmul(qk_ps[:, z * TOK:(z + 1) * TOK], t["wqk"][:, z, :], win[:, i % 2, :], start=True, stop=True)
                m.then_inc(qk_done, 1)

            def step(i, Wd, w):
                (i0, W0), W1, W2 = newest(i, Wd), Wd - 1, Wd - 2
                has0, has1, has2 = i != NWIN, 1 <= i <= NWIN, i >= 2
                b0, b1 = i % 2, (i - 1) % 2

                def scores_for_max(h):
                    if not has0:
                        return
                    pe.wait_ge(kz_ready, BASE + HEADS * W0 + (h + 1))
                    pe.wait_ge(max_done, BASE + HEADS * W0 + (h - 1))
                    for j in range(2):
                        m = pe.matmul(psum[:, h % 2, TOK * j:TOK * j + TOK], qb[:, b0, 128 * j:128 * j + 128],
                                      kb[:, b0, h, :], start=True, stop=True)
                    m.then_inc(s1_done, 1)

                def scores(h):
                    if not has1:
                        return
                    pe.wait_ge(exp_done, BASE + HEADS * W1 + (h - 1))
                    for j in range(2):
                        m = pe.matmul(psum[:, 2 + h % 2, TOK * j:TOK * j + TOK],
                                      kz[:, b1, h, 128 * j:128 * j + 128], qaug[:], start=True, stop=True)
                    m.then_inc(s2_done, 1)

                def values(h):
                    if not has1:
                        return
                    pe.wait_ge(exp_done, BASE + HEADS * W1 + (h + 1))
                    for j in range(2):
                        o = (j * HEADS + h) * VW
                        for z in range(2):
                            e = z * TOK + 128 * j
                            m = pe.matmul(pv_ps[:, o:o + VW], E[:, b1, h, e:e + 128], vaug[:, b1, z, h, :],
                                          start=(z == 0), stop=(z == 1))
                    if h == HEADS - 1:
                        m.then_inc(pv_done, 1)

                scores_for_max(0)
                if has0:
                    pe.wait_ge(qaug_done, BASE + W0)
                    for j in range(2):
                        m = pe.matmul(vt_ps[:, j * C:(j + 1) * C], win[:, b0, 128 * j:128 * j + 128], t["wv"][:], start=True, stop=True)
                    m.then_inc(v_done, 1)
                if has1:
                    pe.wait_ge(qaug_done, BASE + W1 + 1)
                scores(0)
                scores_for_max(1)
                if has2:
                    pe.wait_ge(norm_done, BASE + W2 + 1)
                    pe.wait_ge(added, BASE + W2)
                    for j in range(2):
                        m = pe.matmul(pr_ps[0:C, 128 * j:128 * j + 128], on[:, j, :], t["eye"][:], start=True, stop=True)
                    m.then_inc(ot_done, 1)
                scores(1)
                scores_for_max(2)
                if i == NWIN:
                    queries_and_keys(0, Wd)
                elif i0 < NWIN - 1:
                    queries_and_keys(i0 + 1, W0 + 1)
                scores(2)
                scores_for_max(3)
                if has2:
                    pe.wait_ge(ot_out, BASE + W2 + 1)
                    pe.matmul(pr_ps[0:C, 0:TOK], t["wproj"][:], ot[:], start=True, stop=True).then_inc(proj_done, 1)
                if has1:
                    pe.wait_ge(norm_done, BASE + W1)
                values(0)
                scores(3)
                values(1)
                if has0:
                    pe.wait_ge(max_done, BASE + HEADS * W0 + HEADS)
                    pe.wait_ge(v_out, BASE + W0 + 1)
                    for j in range(2):
                        m = pe.matmul(vt_ps[:, 128 * j:128 * j + 128], mz[:, b0, j, :], t["neg_eye"][:], start=True, stop=True)
                    m.then_inc(t_done, 1)
                values(2)
                values(3)

            def body(n, r, last, b):
                each_step(pe, n, step)

            queries_and_keys(0, 0)
            step(0, 0, 0)
            each_band(pe, body)

        @block.vector
        def _(dve):
            def start(b):
                dve.wait_ge(xg_parts, BASE + b * ((bands + 1) * PIECES))
                for to, of in ((scale, "gn_scale"), (shift, "out_shift")):
                    dve.tensor_copy(to[:], t[of][:, bass.ds(b, 1)]).then_inc(batch_set, 1)

            def maxima(i, h, Wd):
                dve.wait_ge(s1_done, BASE + HEADS * Wd + (h + 1))
                dve.tensor_reduce(mz[:, i % 2, :, 32 * h + DQ], psum[:, h % 2, :].rearrange("p (j m) -> p j m", m=TOK),
                                  AX.X, ALU.max).then_inc(max_done, 1)

            def values_and_maxima(i, Wd):
                before = Wd if i == 0 else Wd - 1
                dve.wait_ge(t_done, BASE + before)
                maxima(i, 0, Wd)
                dve.wait_ge(v_done, BASE + Wd + 1)
                dve.wait_ge(pv_done, BASE + before)
                dve.tensor_copy(vaug[:, i % 2, :, :, 0:DV].rearrange("p j h d -> p (j h) d"),
                                vt_ps[:, 0:2 * C].rearrange("p (a d) -> p a d", d=DV)).then_inc(v_out, 1)
                for h in range(1, HEADS):
                    maxima(i, h, Wd)

            def queries_less_maxima(i, Wd):
                dve.wait_ge(t_done, BASE + Wd + 1)
                dve.tensor_tensor(qaug[:], vt_ps[:, 0:TOK], q[:, i % 2, :], ALU.add).then_inc(qaug_done, 1)

            def body(n, r, last, b):
                def sum_columns(first, end, windows):
                    dve.wait_ge(added, BASE + windows)
                    dve.wait_ge(xg_scaled, BASE + 3 * n + 3)
                    o, a, g = (tile[:].rearrange("p (r c) -> p r c", c=W)[:, :, first:end] for tile in (out, acc, xg))
                    dve.tensor_tensor(o, a, g, ALU.add).then_inc(summed, 1)

                def step(i, Wd, w):
                    W1, W2 = Wd - 1, Wd - 2
                    i0, W0 = newest(i, Wd)
                    if i != NWIN:
                        values_and_maxima(i0, W0)
                    if i >= 2:
                        if i == 2:
                            dve.wait_ge(acc_ready, BASE + n + 1)
                        dve.wait_ge(proj_done, BASE + W2 + 1)
                        a = window(acc, w - 2)
                        dve.tensor_tensor(a, pr_ps[0:C, 0:TOK].rearrange("p (r c) -> p r c", c=PS), a, ALU.add).then_inc(added, 1)
                    if i == NWIN:
                        dve.wait_ge(stored, 16 * n)
                        sum_columns(0, LAST - 2, W2)
                    if i == NWIN + 1:
                        sum_columns(LAST - 2, W, W2 + 1)
                    if i != NWIN:
                        queries_less_maxima(i0, W0)
                    if i <= NWIN:
                        dve.wait_ge(pv_done, BASE + W1 + 1)
                        o = pv_ps[:, 0:8 * VW].rearrange("p (a d) -> p a d", d=VW)
                        dve.reciprocal(rden[:], o[:, :, DV]).then_inc(rden_done, 1)
                        dve.wait_ge(rden_done, BASE + W1 + 1)
                        dve.tensor_tensor(on[:].rearrange("p j (h d) -> p (j h) d", d=DV), o[:, :, 0:DV],
                                          rden[:].unsqueeze(2).to_broadcast([128, 8, DV]), ALU.mult).then_inc(norm_done, 1)
                    if i == NWIN - 2:
                        dve.wait_ge(xg_parts, BASE + PIECES * n + PIECES)
                        if last:
                            dve.tensor_scalar(xg[:, 0:STEP * W], xg[:, 0:STEP * W], 2.0, None, ALU.mult).then_inc(xg_scaled, 1)
                        else:
                            dve.tensor_scalar(xg[:, 0:2 * W], xg[:, 0:2 * W], t["first_rows_inverse"][:, bass.ds(r, 1)], None,
                                              ALU.mult).then_inc(xg_scaled, 1)
                    if i == NWIN - 1:
                        dve.wait_ge(xg_scaled, BASE + 3 * n + 1)
                        for part in shared_columns(xg):
                            dve.tensor_scalar(part, part, 2.0, None, ALU.mult).then_inc(xg_scaled, 1)
                each_step(dve, n, step)
                dve.wait_ge(summed, BASE + 2 * n + 2)
                if last:
                    dve.tensor_scalar(out[:, 0:STEP * W], out[:, 0:STEP * W], 0.5, None, ALU.mult).then_inc(out_rows, 1)
                else:
                    dve.tensor_scalar(out[:, 0:2 * W], out[:, 0:2 * W], t["first_rows"][:, bass.ds(r, 1)], None, ALU.mult).then_inc(out_rows, 1)

            values_and_maxima(0, 0)
            queries_less_maxima(0, 0)
            each_band(dve, body, start)


def attention_tables(nc, ctx):
    shapes = {"mean_var": ([C, B, 2], F32), "wqk": ([C, 2, 128], F32), "wv": ([C, C], F32), "wproj": ([C, C], F32),
              "eye": ([128, 128], F32), "neg_eye": ([128, 128], BF16), "centre": ([C, C], F32), "head_rows": ([128, HEADS], F32),
              "first_rows": ([C, NWIN], F32),
              "first_rows_inverse": ([C, NWIN], F32), "ones": ([C, 1], F32), "zero": ([C, 1], F32), "one": ([C, 1], F32), "eps5": ([128, 1], F32),
              "qk_bias": ([128, 2], F32), "gn_scale": ([C, B], F32), "gn_shift": ([C, B], F32), "cen_shift": ([C, B], F32),
              "out_shift": ([C, B], F32), "cen_w": ([C, B, C], F32), "mz": ([128, 2, 2, 128], BF16),
              "vaug": ([128, 2, 2, HEADS, DV + 1], F32), "acc": ([C, PS * W], F32)}
    return {k: ctx.enter_context(nc.sbuf_tensor("t_" + k, s, d)) for k, (s, d) in shapes.items()}
CHK = 512
FG = 16
BLK = 32
OWN = 28
NBLK = 9
TAPS = 5
CPB = 128 // BLK
NGRP = MLP // CPB
UR = OWN // 2


def conv_constants():
    taps = np.zeros((128, TAPS, 128), np.float32)
    for c in range(CPB):
        for m in range(BLK):
            for dy in range(TAPS):
                k = m + dy - TAPS // 2
                if 0 <= k < BLK:
                    taps[c * BLK + k, dy, c * BLK + m] = 1.0
    return {"k_taps": taps}


def fc1(nc, p, x2, ydr, groups=B * H // FG):
    NTOK = FG * W
    NCK = NTOK // CHK
    NT = NTOK // 128
    with ExitStack() as ctx:
        def sb(name, shape, dt=F32):
            return ctx.enter_context(nc.sbuf_tensor("f1_" + name, shape, dt))

        def sem(name):
            return ctx.enter_context(nc.semaphore("f1_" + name))

        w1 = sb("w1", [C, MLP])
        n2 = sb("n2", [C, 2])
        b1 = sb("b1", [C, 2])
        bias = sb("bias", [C, 2])
        eye = sb("eye", [128, 128])
        centre = sb("centre", [C, C])
        ones = sb("ones", [C, 1])
        eps = sb("eps", [128, 1])
        xin = sb("xin", [C, 2, NTOK])
        z = sb("z", [C, 2, NTOK])
        sq = sb("sq", [C, 2, CHK])
        sd = sb("sd", [128, NT])
        rs = sb("rs", [128, NT])
        yo = sb("yo", [C, 4, 2, CHK])
        psum = ctx.enter_context(nc.psum_tensor("f1_ps", [128, 8, 512], F32))
        w_loaded, filled, w_set, b_done = sem("w_loaded"), sem("filled"), sem("w_set"), sem("b_done")
        x_loaded = [sem(f"x_loaded{i}") for i in range(2)]
        stored = [sem(f"stored{i}") for i in range(4)]
        cen_done, cs_done, sq_done, var_done, sd_done, rs_done, bc_done, z_done, f_done, y_done = (
            sem(s) for s in ("cen_done", "cs_done", "sq_done", "var_done", "sd_done", "rs_done", "bc_done", "z_done", "f_done", "y_done"))
        block = ctx.enter_context(nc.Block())
        per = H // FG

        def steps(eng, step):
            step(0, 0, True, False)
            with eng.Fori(0, (groups - 2) // 2) as j:
                step(1, 2 * j + 1, True, True)
                step(0, 2 * j + 2, True, True)
            step(1, groups - 1, True, True)
            step(0, groups, False, True)

        def rows_of(a, k):
            return a[bass.ds(k // per, 1), :, bass.ds((k % per) * FG, FG), :].rearrange("a c r w -> (a c) (r w)")

        @block.gpsimd
        def _(pool):
            pool.memset(ones[:], 1.0 / C).then_inc(filled, 1)
            pool.memset(eps[:], 1e-5).then_inc(filled, 1)
            with pool.Fori(0, groups) as k:
                for c in range(NCK):
                    pool.wait_ge(y_done, k * NCK + (c + 1))
                    dst = ydr[:, bass.ds((k % per) * FG + 2 * c, 2), bass.ds(k // per, 1), :]
                    for h in range(2):
                        pool.dma_start(dst[h * C:(h + 1) * C].rearrange("c r b w -> c r (b w)"),
                                       yo[:, c % 4, h, :].rearrange("c (r w) -> c r w", w=W)).then_inc(stored[c % 4], 16)
            for i in range(4):
                pool.wait_ge(stored[i], 64 * groups)

        @block.sync
        def _(sp):
            sp.dma_start(w1[:], p["fc1_w"]).then_inc(w_loaded, 16)
            sp.dma_start(n2[:, 0:1], p["norm2_w"].rearrange("(c a) -> c a", a=1)).then_inc(w_loaded, 16)
            sp.dma_start(n2[:, 1:2], p["norm2_b"].rearrange("(c a) -> c a", a=1)).then_inc(w_loaded, 16)
            for h in range(2):
                sp.dma_start(b1[:, h:h + 1], p["fc1_b"][h * C:(h + 1) * C].rearrange("(c a) -> c a", a=1)).then_inc(w_loaded, 16)
            sp.dma_start(eye[:], p["k_eye"]).then_inc(w_loaded, 16)
            sp.dma_start(centre[:], p["k_centre"]).then_inc(w_loaded, 16)
            for i in range(2):
                sp.dma_start(xin[:, i, :], rows_of(x2, i)).then_inc(x_loaded[i], 16)
            with sp.Fori(0, groups // 2 - 1) as j:
                for u in range(2):
                    k = 2 * j + u
                    sp.wait_ge(cen_done, k * NCK + NCK)
                    sp.dma_start(xin[:, u, :], rows_of(x2, 2 * j + (u + 2))).then_inc(x_loaded[u], 16)

        @block.tensor
        def _(pe):
            pe.wait_ge(w_loaded, 16 * 7)
            pe.wait_ge(filled, 2)
            for h in range(2):
                m = pe.matmul(psum[0:C, 3, h:h + 1], w1[:, h * C:(h + 1) * C], n2[:, 1:2], start=True, stop=True)
            m.then_inc(b_done, 1)
            pe.wait_ge(w_set, 2)

            def step(u, k, stats, products):
                base, was = k * NCK, (k - 1) * NCK
                o = 1 - u

                def variance(c):
                    pe.wait_ge(sq_done, base + (c + 1))
                    if c == 0:
                        pe.wait_ge(sd_done, k)
                    for s in range(CHK // 128):
                        m = pe.matmul(psum[:, 2, 4 * c + s:4 * c + s + 1], sq[:, c % 2, 128 * s:128 * s + 128], ones[:], start=True, stop=True)
                    m.then_inc(var_done, 1)

                def product(c):
                    pe.wait_ge(z_done, was + (c + 1))
                    for h in range(2):
                        bank = 4 + 2 * (c % 2) + h
                        m = pe.matmul(psum[0:C, bank, :], w1[:, h * C:(h + 1) * C], z[:, o, c * CHK:(c + 1) * CHK], start=True, stop=True)
                    m.then_inc(f_done, 1)

                if stats:
                    pe.wait_ge(x_loaded[u], 8 * (k - u) + 16)
                for c in range(NCK):
                    if stats:
                        if c >= 2 or products:
                            pe.wait_ge(cs_done, base + (c - 1))
                        pe.matmul(psum[0:C, c % 2, :], centre[:], xin[:, u, c * CHK:(c + 1) * CHK], start=True, stop=True).then_inc(cen_done, 1)
                        if c >= 1:
                            variance(c - 1)
                    if products:
                        if c == 0:
                            pe.wait_ge(rs_done, k)
                            pe.wait_ge(z_done, was)
                        else:
                            pe.wait_ge(z_done, was + c)
                        for s in range(CHK // 128):
                            m = pe.matmul(psum[0:C, 3, 128 * s:128 * s + 128], rs[:, 4 * c + s:4 * c + s + 1].to_broadcast([128, C]), eye[:],
                                          start=True, stop=True)
                        m.then_inc(bc_done, 1)
                        if c >= 1:
                            pe.wait_ge(y_done, was + max(c - 2, 0))
                            product(c - 1)
                if stats:
                    variance(NCK - 1)
                if products:
                    pe.wait_ge(y_done, was + (NCK - 2))
                    product(NCK - 1)
            steps(pe, step)

        @block.scalar
        def _(act):
            def step(u, k, stats, products):
                base, was = k * NCK, (k - 1) * NCK

                def gelu(c):
                    act.wait_ge(f_done, was + (c + 1))
                    act.wait_ge(stored[c % 4], 64 * (k - 1) + 32 * (c // 4))
                    for h in range(2):
                        i = act.activation(yo[:, c % 4, h, :], psum[0:C, 4 + 2 * (c % 2) + h, :], ACT.Gelu, bias=bias[:, h:h + 1])
                    i.then_inc(y_done, 1)

                for c in range(NCK):
                    if stats:
                        act.wait_ge(cen_done, base + (c + 1))
                        act.activation(z[:, u, c * CHK:(c + 1) * CHK], psum[0:C, c % 2, :], ACT.Copy).then_inc(cs_done, 1)
                    if products and c >= 1:
                        gelu(c - 1)
                if products:
                    gelu(NCK - 1)
                if stats:
                    act.wait_ge(var_done, base + NCK)
                    act.activation(sd[:], psum[:, 2, 0:NT], ACT.Sqrt, bias=eps[:]).then_inc(sd_done, 1)
            act.wait_ge(filled, 2)
            steps(act, step)

        @block.vector
        def _(dve):
            dve.wait_ge(b_done, 1)
            dve.wait_ge(w_loaded, 16 * 7)
            dve.tensor_tensor(bias[:], psum[0:C, 3, 0:2], b1[:], ALU.add).then_inc(w_set, 1)
            dve.tensor_scalar(w1[:], w1[:], n2[:, 0:1], None, ALU.mult).then_inc(w_set, 1)

            def step(u, k, stats, products):
                base, was = k * NCK, (k - 1) * NCK
                for c in range(NCK):
                    if stats:
                        dve.wait_ge(cs_done, base + (c + 1))
                        if c >= 2 or products:
                            dve.wait_ge(var_done, base + (c - 1))
                        zc = z[:, u, c * CHK:(c + 1) * CHK]
                        dve.tensor_tensor(sq[:, c % 2, :], zc, zc, ALU.mult).then_inc(sq_done, 1)
                    if products:
                        dve.wait_ge(bc_done, was + (c + 1))
                        zc = z[:, 1 - u, c * CHK:(c + 1) * CHK]
                        dve.tensor_tensor(zc, psum[0:C, 3, :], zc, ALU.mult).then_inc(z_done, 1)
                if stats:
                    dve.wait_ge(sd_done, k + 1)
                    if products:
                        dve.wait_ge(bc_done, base)
                    dve.reciprocal(rs[:], sd[:]).then_inc(rs_done, 1)
            steps(dve, step)


def conv(nc, p, ydr, sdr, pairs=NGRP // 2):
    with ExitStack() as ctx:
        def sb(name, shape, dt=F32):
            return ctx.enter_context(nc.sbuf_tensor("cv_" + name, shape, dt))

        def sem(name):
            return ctx.enter_context(nc.semaphore("cv_" + name))

        NS = 3
        PAD = TAPS // 2
        taps = sb("taps", [128, TAPS, 128])
        wd = sb("wd", [128, NGRP + 1, TAPS * TAPS])
        bd = sb("bd", [128, NGRP + 1])
        bcur = sb("bcur", [128, 2])
        band = sb("band", [128, 2, TAPS, 128])
        part = sb("part", [128, TAPS, 128])
        yin = sb("yin", [128, NS, B, W + 2 * PAD])
        gl = sb("gl", [128, NS, B * W])
        so = sb("so", [128, NS, B * W])
        psum = ctx.enter_context(nc.psum_tensor("cv_ps", [128, NS, 512], F32))
        w_loaded, filled, chain = sem("w_loaded"), sem("filled"), sem("chain")
        loaded = [sem(f"loaded{i}") for i in range(NS)]
        stored = [sem(f"stored{i}") for i in range(NS)]
        conv_done, gl_done = sem("conv_done"), sem("gl_done")
        summed = sem("summed")
        block = ctx.enter_context(nc.Block())
        SPB = 2 * NBLK
        SPS = SPB // NS
        LINKS = 2 * TAPS - 1

        def steps(eng, step):
            with eng.Fori(0, pairs) as j:
                for gg in range(2):
                    for t in range(NBLK):
                        step(j, gg, t, gg * NBLK + t)

        @block.sync
        def _(sp):
            sp.dma_start(taps[:], p["k_taps"]).then_inc(w_loaded, 16)
            sp.wait_ge(filled, 2)
            for c in range(CPB):
                rows = slice(c * BLK, (c + 1) * BLK)
                sp.dma_start(wd[rows, 0:NGRP, :], p["dw_w"].rearrange("(g c) a u v -> c a g (u v)", c=CPB)[c].to_broadcast([BLK, NGRP, TAPS * TAPS])
                             ).then_inc(w_loaded, 16)
                sp.dma_start(bd[rows, 0:NGRP], p["dw_b"].rearrange("(g c a) -> c a g", c=CPB, a=1)[c].to_broadcast([BLK, NGRP]),
                             allow_slow_non_contiguous=True).then_inc(w_loaded, 16)

            def step(j, gg, t, s):
                b = s % NS
                sp.wait_ge(summed, j * SPB + (s + 1))
                src = ydr[bass.ds(j * (2 * CPB) + gg * CPB, CPB), t * OWN:t * OWN + BLK]
                for i in range(B):
                    sp.dma_start(yin[:, b, i, PAD:PAD + W], src[:, :, i, :]).then_inc(loaded[b], 16)
            steps(sp, step)

        @block.gpsimd
        def _(pool):
            pool.memset(wd[:, NGRP, :], 0.0).then_inc(filled, 1)
            pool.memset(bd[:, NGRP:], 0.0).then_inc(filled, 1)

            def step(j, gg, t, s):
                pool.wait_ge(summed, j * SPB + (s + 1 + NS))
                dst = sdr[t, bass.ds(j * (2 * CPB) + gg * CPB, CPB)]
                pool.dma_start(dst.rearrange("c k b w -> (c k) (b w)"), so[:, s % NS, :]).then_inc(stored[s % NS], 16)
            steps(pool, step)
            for i in range(NS):
                pool.wait_ge(stored[i], 16 * pairs * SPS)

        @block.tensor
        def _(pe):
            def step(j, gg, t, s):
                b = s % NS
                if t == 0:
                    pe.wait_ge(chain, j * (2 * LINKS) + (gg + 1) * LINKS)
                pe.wait_ge(loaded[b], j * (32 * SPS) + 32 * (s // NS + 1))
                for dx in range(TAPS):
                    m = pe.matmul(psum[:, b, :], band[:, gg, dx, :], yin[:, b, :, dx:dx + W], start=(dx == 0), stop=(dx == TAPS - 1))
                m.then_inc(conv_done, 1)
            steps(pe, step)

        @block.scalar
        def _(act):
            def step(j, gg, t, s):
                b = s % NS
                act.wait_ge(conv_done, j * SPB + (s + 1))
                act.activation(gl[:, b, :], psum[:, b, :], ACT.Gelu, bias=bcur[:, gg:gg + 1]).then_inc(gl_done, 1)
            steps(act, step)

        @block.vector
        def _(dve):
            for i in range(NS):
                dve.memset(yin[:, i, :, 0:PAD], 0.0)
                dve.memset(yin[:, i, :, PAD + W:], 0.0).then_inc(summed, 1)
            dve.wait_ge(w_loaded, 16 * (2 * CPB + 1))

            def set_band(g, to, done):
                dve.tensor_scalar(bcur[:, to:to + 1], bd[:, bass.ds(g, 1)], 0.0, None, ALU.add)
                for dy in range(TAPS):
                    tap = taps[:, dy, :].unsqueeze(1).to_broadcast([128, TAPS, 128])
                    w = wd[:, bass.ds(g, 1), dy * TAPS:(dy + 1) * TAPS].rearrange("p a u -> p (a u)").unsqueeze(2).to_broadcast([128, TAPS, 128])
                    if dy:
                        dve.wait_ge(chain, done + (2 * dy - 1))
                    dve.tensor_tensor(part[:] if dy else band[:, to], tap, w, ALU.mult).then_inc(chain, 1)
                    if dy:
                        dve.wait_ge(chain, done + 2 * dy)
                        dve.tensor_tensor(band[:, to], band[:, to], part[:], ALU.add).then_inc(chain, 1)

            set_band(0, 0, 0)

            def step(j, gg, t, s):
                b = s % NS
                if t == 1:
                    dve.wait_ge(conv_done, j * SPB + gg * NBLK)
                    set_band(j * 2 + (gg + 1), 1 - gg, j * (2 * LINKS) + (gg + 1) * LINKS)
                dve.wait_ge(gl_done, j * SPB + (s + 1))
                dve.wait_ge(stored[b], j * (16 * SPS) + 16 * (s // NS))
                dve.tensor_tensor(so[:, b, :].rearrange("p (i w) -> p i w", w=W), gl[:, b, :].rearrange("p (i w) -> p i w", w=W),
                                  yin[:, b, :, PAD:PAD + W], ALU.add).then_inc(summed, 1)
            steps(dve, step)


def fc2(nc, p, x, x2, sdr, x1, tab, edges, batches=B, blocks=NBLK):
    rows = 2 if edges else UR
    n_ck = 2 * B if edges else rows * W // CHK
    NTOK = n_ck * CHK
    name = "fe_" if edges else "f2_"
    with ExitStack() as ctx:
        def sb(nm, shape, dt=F32):
            return ctx.enter_context(nc.sbuf_tensor(name + nm, shape, dt))

        def sem(nm):
            return ctx.enter_context(nc.semaphore(name + nm))

        NB = 1 if edges else 2
        w2 = sb("w2", [C, 2, C])
        b2 = sb("b2", [C, 1])
        st = sb("st", [C, NB, 2, NTOK])
        xa = sb("xa", [C, NB, NTOK])
        xb = sb("xb", [C, NB, NTOK])
        psum = ctx.enter_context(nc.psum_tensor(name + "ps", [128, n_ck, 512], F32))
        w_loaded = sem("w_loaded")
        loaded = [sem(f"loaded{i}") for i in range(NB)]
        stored = [sem(f"stored{i}") for i in range(NB)]
        xs_done, f_done, sums_done, squares_done = sem("xs_done"), sem("f_done"), sem("sums_done"), sem("squares_done")
        x1_done = sem("x1_done")
        block = ctx.enter_context(nc.Block())
        count = 1 if edges else batches * blocks * 2
        side = [(b, e) for b in range(B) for e in range(2)]

        def units(eng, unit):
            if edges:
                unit(0, 0, None, None)
                return
            with eng.Fori(0, batches * blocks) as i:
                for u in range(2):
                    unit(2 * i + u, u, i // blocks, i % blocks)

        def image(a, b, t, u):
            return a[bass.ds(b, 1), :, bass.ds(t * OWN + (2 + UR * u), UR), :].rearrange("a c r w -> (a c) (r w)")

        @block.sync
        def _(sp):
            sp.dma_start(w2[:], p["fc2_w"].rearrange("(h c) o -> c h o", h=2)).then_inc(w_loaded, 16)
            sp.dma_start(b2[:], p["fc2_b"].rearrange("(c a) -> c a", a=1)).then_inc(w_loaded, 16)

            def unit(n, u, b, t):
                if edges:
                    for i, (b, e) in enumerate(side):
                        at = slice(i * CHK, (i + 1) * CHK)
                        r0, k0, tt = (H - 2, BLK - 2, NBLK - 1) if e else (0, 0, 0)
                        for h in range(2):
                            sp.dma_start(st[:, 0, h, at].rearrange("c (r w) -> c r w", w=W), sdr[tt, h * C:(h + 1) * C, k0:k0 + 2, b, :]).then_inc(loaded[0], 16)
                        sp.dma_start(xa[:, 0, at], x2[b, :, r0:r0 + 2, :].rearrange("c r w -> c (r w)")).then_inc(loaded[0], 16)
                        sp.dma_start(xb[:, 0, at], x[b, :, r0:r0 + 2, :].rearrange("c r w -> c (r w)")).then_inc(loaded[0], 16)
                    return
                sp.wait_ge(stored[u], 8 * (n - u))
                for h in range(2):
                    src = sdr[bass.ds(t, 1), h * C:(h + 1) * C, 2 + UR * u:2 + UR * (u + 1), bass.ds(b, 1), :]
                    sp.dma_start(st[:, u, h, :].rearrange("c (r w) -> c r w", w=W), src.rearrange("a c r b w -> (a c) r (b w)")).then_inc(loaded[u], 16)
                sp.dma_start(xa[:, u, :], image(x2, b, t, u)).then_inc(loaded[u], 16)
                sp.dma_start(xb[:, u, :], image(x, b, t, u)).then_inc(loaded[u], 16)
            units(sp, unit)

        n_loads = 16 if edges else 4

        def wait_loaded(eng, n, u):
            eng.wait_ge(loaded[u], (n - u) * (8 * n_loads) + 16 * n_loads)

        @block.gpsimd
        def _(pool):
            def unit(n, u, b, t):
                wait_loaded(pool, n, u)
                pool.tensor_tensor(xa[:, u, :], xa[:, u, :], xb[:, u, :], ALU.add).then_inc(xs_done, 1)
            units(pool, unit)

        @block.tensor
        def _(pe):
            pe.wait_ge(w_loaded, 32)

            def unit(n, u, b, t):
                wait_loaded(pe, n, u)
                for c in range(n_ck):
                    pe.wait_ge(x1_done, n * n_ck + (c + 1))
                    for h in range(2):
                        m = pe.matmul(psum[0:C, c, :], w2[:, h, :], st[:, u, h, c * CHK:(c + 1) * CHK], start=(h == 0), stop=(h == 1))
                    m.then_inc(f_done, 1)
            units(pe, unit)

        @block.vector
        def _(dve):
            dve.sem_inc(x1_done, n_ck)
            dve.wait_ge(w_loaded, 32)

            def unit(n, u, b, t):
                dve.wait_ge(xs_done, n + 1)
                for c in range(n_ck):
                    dve.wait_ge(f_done, n * n_ck + (c + 1))
                    xc = xa[:, u, c * CHK:(c + 1) * CHK]
                    dve.scalar_tensor_tensor(out=xc, in0=psum[0:C, c, :], scalar=b2[:, 0:1], in1=xc, op0=ALU.add, op1=ALU.add).then_inc(x1_done, 1)
                dve.wait_ge(x1_done, n * n_ck + 2 * n_ck)
                sums = tab["row_sums"]
                if edges:
                    for i, (b, e) in enumerate(side):
                        r0 = b * H + (H - 2 if e else 0)
                        dve.tensor_reduce(sums[:, r0:r0 + 2, :], xa[:, 0, i * CHK:(i + 1) * CHK].rearrange("c (r q w) -> c r q w", r=2, w=64),
                                          AX.X, ALU.add).then_inc(sums_done, 1)
                else:
                    dve.tensor_reduce(sums[:, bass.ds(b * H + t * OWN + (2 + UR * u), UR), :],
                                      xa[:, u, :].rearrange("c (r q w) -> c r q w", q=4, w=64), AX.X, ALU.add).then_inc(sums_done, 1)
            units(dve, unit)

        @block.scalar
        def _(act):
            def unit(n, u, b, t):
                act.wait_ge(x1_done, n * n_ck + 2 * n_ck)
                if edges:
                    for i, (b, e) in enumerate(side):
                        at = slice(i * CHK, (i + 1) * CHK)
                        act.activation(xb[:, 0, at], xa[:, 0, at], ACT.Square,
                                       accum_out=tab["squares"][:, b, 2 * NBLK + e:2 * NBLK + e + 1]).then_inc(squares_done, 1)
                    act.wait_ge(squares_done, len(side))
                    act.wait_ge(sums_done, len(side))
                    for i, (b, e) in enumerate(side):
                        r0 = H - 2 if e else 0
                        act.dma_start(x1[b, :, r0:r0 + 2, :].rearrange("c r w -> c (r w)"), xa[:, 0, i * CHK:(i + 1) * CHK]).then_inc(stored[0], 16)
                    act.wait_ge(stored[0], 16 * len(side))
                    return
                act.activation(xb[:, u, :], xa[:, u, :], ACT.Square,
                               accum_out=tab["squares"][:, bass.ds(b, 1), bass.ds(t * 2 + u, 1)].rearrange("p a b -> p (a b)")).then_inc(squares_done, 1)
                act.wait_ge(squares_done, n + 1)
                act.wait_ge(sums_done, n + 1)
                act.dma_start(image(x1, b, t, u), xa[:, u, :]).then_inc(stored[u], 16)
            units(act, unit)
            if not edges:
                for u in range(2):
                    act.wait_ge(stored[u], 16 * batches * blocks)
CH_HEADS, CH_DIM = 4, 24
NCTR = 4
EM = CH_HEADS * NCTR
REG = H // 2
NREG = B * 4
NFC = 2 * C + EM


def cluster_constants():
    heads = np.zeros((C, CH_HEADS), np.float32)
    for e in range(CH_HEADS):
        heads[e * CH_DIM:(e + 1) * CH_DIM, e] = 1.0
    return {"k_heads": heads, "k_same_head": heads @ heads.T,
            "k_own_channels": np.repeat(heads.T, NCTR, axis=0).copy()}


def cluster_tables(nc, ctx):
    shapes = {"rhs": [C + 1, NREG, NFC], "value_centres": [EM, NREG, C], "eye": [128, 128], "proj": [C, C], "proj_b": [C, 1],
              "beta": [128, 1], "own_channels": [EM, C]}
    return {k: ctx.enter_context(nc.sbuf_tensor("c_" + k, s, F32)) for k, s in shapes.items()}


def cluster_setup(nc, p, tab, t):
    with ExitStack() as ctx:
        def sb(name, shape, dt=F32):
            return ctx.enter_context(nc.sbuf_tensor("cs_" + name, shape, dt))

        NBK = 16
        bsum = sb("bsum", [C, B, NBK])
        stat = sb("stat", [C, 2, B])
        avg = sb("avg", [C, 2, B])
        sq = sb("sq", [C, B])
        sd = sb("sd", [C, B])
        eps = sb("eps", [C, 1])
        scale = sb("scale", [C + 1, B])
        shift = sb("shift", [C, B])
        group = sb("group", [C, C])
        heads = sb("heads", [C, CH_HEADS])
        same = sb("same", [C, C])
        fv_t = sb("fv_t", [C, 2 * C])
        fv_b = sb("fv_b", [C + 1, 2 * C])
        f_col = sb("f_col", [C, 1])
        f_nat = sb("f_nat", [C, B, C + 1])
        alpha = sb("alpha", [C, 1])
        wfv = sb("wfv", [C + 1, B, 2 * C])
        xm = sb("xm", [C + 1, B, NBK])
        xmq = sb("xmq", [C + 1, NREG, CH_HEADS, NCTR])
        cf = sb("cf", [C, B, NBK])
        cs = sb("cs", [C, B, NBK])
        cn = sb("cn", [C, B, NBK])
        ctr = sb("ctr", [C, NREG, CH_HEADS, NCTR])
        psum = ctx.enter_context(nc.psum_tensor("cs_ps", [128, 8, 512], F32))
        loaded = ctx.enter_context(nc.semaphore("cs_loaded"))
        ones_set = ctx.enter_context(nc.semaphore("cs_ones_set"))
        dch = ctx.enter_context(nc.semaphore("cs_vector_done"))
        pch = ctx.enter_context(nc.semaphore("cs_products_done"))
        ach = ctx.enter_context(nc.semaphore("cs_roots_done"))
        stage = ctx.enter_context(nc.semaphore("cs_stage"))
        block = ctx.enter_context(nc.Block())
        loads = [(group[:], p["k_group"]), (heads[:], p["k_heads"]), (same[:], p["k_same_head"]),
                 (fv_t[:, 0:C], p["f_wt"]), (fv_t[:, C:], p["v_wt"]),
                 (fv_b[C:C + 1, 0:C], p["f_b"].rearrange("(a c) -> a c", a=1)),
                 (fv_b[C:C + 1, C:], p["v_b"].rearrange("(a c) -> a c", a=1)),
                 (f_col[:], p["f_b"].rearrange("(c a) -> c a", a=1)),
                 (f_nat[:, 0, 0:C], p["f_w"]), (f_nat[:, 1, 0:C], p["f_w"]),
                 (alpha[:], p["sim_alpha"].partition_broadcast(C)),
                 (t["beta"][:], p["sim_beta"].partition_broadcast(128)),
                 (t["eye"][:], p["k_eye"]), (t["proj"][:], p["proj_wt"]),
                 (t["proj_b"][:], p["proj_b"].rearrange("(c a) -> c a", a=1)), (t["own_channels"][:], p["k_own_channels"])]

        @block.sync
        def _(sp):
            for to, of in loads:
                sp.dma_start(to, of).then_inc(loaded, 16)

        @block.gpsimd
        def _(pool):
            pool.memset(eps[:], 1e-5).then_inc(ones_set, 1)
            pool.memset(scale[C:C + 1, :], 1.0).then_inc(ones_set, 1)
            pool.memset(xm[C:C + 1, :, :], 1.0).then_inc(ones_set, 1)

        @block.scalar
        def _(act):
            act.wait_ge(ones_set, 3)
            act.wait_ge(stage, 2)
            act.activation(sd[:], sq[:], ACT.Sqrt, bias=eps[:]).then_inc(ach, 1)
            act.wait_ge(pch, 4)
            act.activation(cs[:].rearrange("p b n -> p (b n)"), psum[0:C, 4, 0:B * NBK], ACT.Sqrt).then_inc(ach, 1)

        @block.tensor
        def _(pe):
            pe.wait_ge(loaded, 16 * len(loads))
            pe.wait_ge(stage, 1)
            pe.matmul(psum[0:C, 0, 0:2 * B], group[:], stat[:].rearrange("p a b -> p (a b)"), start=True, stop=True).then_inc(pch, 1)
            pe.wait_ge(stage, 3)
            for b in range(B):
                pe.matmul(psum[C:C + 1, 1, b * 2 * C:(b + 1) * 2 * C], shift[:, b:b + 1], fv_t[:], start=True, stop=True)
            pe.matmul(psum[0:C, 2, 0:B], fv_t[:, 0:C], shift[:], start=True, stop=True).then_inc(pch, 1)
            pe.wait_ge(stage, 4)
            for b in range(B):
                m = pe.matmul(psum[0:C, 3, b * NBK:(b + 1) * NBK], wfv[:, b, 0:C], xm[:, b, :], start=True, stop=True)
            m.then_inc(pch, 1)
            pe.wait_ge(stage, 5)
            pe.matmul(psum[0:C, 4, 0:B * NBK], same[:], cs[:].rearrange("p b n -> p (b n)"), start=True, stop=True).then_inc(pch, 1)
            pe.wait_ge(stage, 6)
            for b in range(B):
                pe.matmul(psum[0:C + 1, 5, b * 4 * EM:(b + 1) * 4 * EM], f_nat[:, b, :],
                          ctr[:, 4 * b:4 * b + 4].rearrange("p q e m -> p (q e m)"), start=True, stop=True)
            for q in range(NREG):
                m = pe.matmul(psum[0:EM, 6 + q // 4, (q % 4) * C:(q % 4 + 1) * C], xmq[:, q].rearrange("p e m -> p (e m)"),
                              wfv[:, q // 4, C:2 * C], start=True, stop=True)
            m.then_inc(pch, 1)

        @block.vector
        def _(dve):
            n = [0]

            def link(ins):
                n[0] += 1
                ins.then_inc(dch, 1)
                dve.wait_ge(dch, n[0])

            def staged():
                dve.sem_inc(stage, 1)

            rows = H // 4
            for b in range(B):
                link(dve.tensor_reduce(bsum[:, b, :].rearrange("p (i j) -> p i j", j=4),
                                       tab["row_sums"][:, b * H:(b + 1) * H, :].rearrange("p (i r) j -> p i j r", r=rows), AX.X, ALU.add))
            link(dve.tensor_reduce(stat[:, 0, :], bsum[:], AX.X, ALU.add))
            link(dve.tensor_reduce(stat[:, 1, :], tab["squares"][:], AX.X, ALU.add))
            link(dve.tensor_scalar(stat[:], stat[:], 1.0 / PIX, None, ALU.mult))
            staged()
            dve.wait_ge(pch, 1)
            link(dve.tensor_copy(avg[:].rearrange("p a b -> p (a b)"), psum[0:C, 0, 0:2 * B]))
            link(dve.tensor_tensor(sq[:], avg[:, 0, :], avg[:, 0, :], ALU.mult))
            link(dve.tensor_tensor(sq[:], avg[:, 1, :], sq[:], ALU.subtract))
            link(dve.tensor_scalar(sq[:], sq[:], 0.0, None, ALU.max))
            staged()
            dve.wait_ge(ach, 1)
            dve.wait_ge(ones_set, 3)
            link(dve.reciprocal(scale[0:C, :], sd[:]))
            link(dve.scalar_tensor_tensor(out=shift[:], in0=avg[:, 0, :], scalar=-1.0, in1=scale[0:C, :], op0=ALU.mult, op1=ALU.mult))
            staged()
            dve.wait_ge(loaded, 16 * len(loads))
            dve.wait_ge(pch, 2)
            for b in range(B):
                link(dve.tensor_scalar(wfv[0:C, b, :], fv_t[:], scale[0:C, b:b + 1], None, ALU.mult))
                link(dve.tensor_tensor(wfv[C:C + 1, b, :], psum[C:C + 1, 1, b * 2 * C:(b + 1) * 2 * C], fv_b[C:C + 1, :], ALU.add))
                link(dve.tensor_tensor(f_nat[:, b, C:C + 1], psum[0:C, 2, b:b + 1], f_col[:], ALU.add))
            link(dve.tensor_scalar(xm[0:C, :, :], bsum[:], 1.0 / (rows * rows), None, ALU.mult))
            staged()
            dve.wait_ge(pch, 3)
            link(dve.tensor_copy(cf[:].rearrange("p b n -> p (b n)"), psum[0:C, 3, 0:B * NBK]))
            link(dve.tensor_tensor(cs[:], cf[:], cf[:], ALU.mult))
            staged()
            dve.wait_ge(ach, 2)
            link(dve.tensor_scalar(cs[:], cs[:], 1e-12, None, ALU.max))
            link(dve.reciprocal(cn[:], cs[:]))
            link(dve.tensor_tensor(cn[:], cn[:], cf[:], ALU.mult))
            link(dve.tensor_scalar(cn[:], cn[:], alpha[:, 0:1], None, ALU.mult))
            for q in range(NREG):
                b, f1, f2 = q // 4, q // 2 % 2, q % 2

                def quarters(a):
                    return a[:, b, :].rearrange("p (i j) -> p i j", j=4)[:, 2 * f1:2 * f1 + 2, 2 * f2:2 * f2 + 2]
                for e in range(CH_HEADS):
                    link(dve.tensor_scalar(ctr[:, q, e, :].rearrange("p (i j) -> p i j", j=2), quarters(cn), heads[:, e:e + 1], None, ALU.mult))
                    link(dve.tensor_copy(xmq[:, q, e, :].rearrange("p (i j) -> p i j", j=2), quarters(xm)))
            staged()
            dve.wait_ge(pch, 5)
            for q in range(NREG):
                b = q // 4
                link(dve.tensor_copy(t["rhs"][:, q, 0:2 * C], wfv[:, b, :]))
                link(dve.tensor_scalar(t["rhs"][:, q, 2 * C:], psum[0:C + 1, 5, q * EM:(q + 1) * EM], scale[:, b:b + 1], None, ALU.mult))
                link(dve.tensor_copy(t["value_centres"][:, q, :], psum[0:EM, 6 + q // 4, (q % 4) * C:(q % 4 + 1) * C]))


def cluster(nc, x1, out, t, halves=B * 2):
    UROWS = 4
    NT = 8
    UT = UROWS * W
    UNITS = REG // UROWS
    SU = 4
    UPS = UNITS // SU
    TPS = UPS * NT
    VC = C + 1
    NQ = TPS * CH_HEADS
    with ExitStack() as ctx:
        def sb(name, shape, dt=F32):
            return ctx.enter_context(nc.sbuf_tensor("cl_" + name, shape, dt))

        def sem(name):
            return ctx.enter_context(nc.semaphore("cl_" + name))

        xu = sb("xu", [C + 1, 2, UT])
        sqf = sb("sqf", [128, 2, 4, C])
        val = sb("val", [128, 2, TPS, VC])
        dots = sb("dots", [128, 2, TPS, EM])
        n2 = sb("n2", [128, 2, NQ])
        nr = sb("nr", [128, NQ])
        rn = sb("rn", [128, NQ])
        sim = sb("sim", [128, NQ, NCTR])
        hit = sb("hit", [128, NQ, NCTR])
        top = sb("top", [128, NQ])
        got = sb("got", [128, NQ])
        sm = sb("sm", [128, 2, TPS, EM])
        smt = sb("smt", [128, UNITS, 128])
        zero = sb("zero", [128, 2 * VC])
        agg = sb("agg", [EM, 2, C])
        den = sb("den", [EM, 2])
        aggt = sb("aggt", [C, NT, 128])
        lhs = sb("lhs", [128, NT, C])
        ou = sb("ou", [C, 2, UT])
        psum = ctx.enter_context(nc.psum_tensor("cl_ps", [128, 8, 512], F32))
        loaded = [sem(f"loaded{i}") for i in range(2)]
        stored = [sem(f"stored{i}") for i in range(2)]
        filled, aggs = sem("filled"), sem("aggs")
        prod_done, sq_done, n2_done = sem("prod_done"), sem("sq_done"), sem("n2_done")
        out_done = sem("out_done")
        rt_done, sim_done, sg_done, sm_done, chain = sem("rt_done"), sem("sim_done"), sem("sg_done"), sem("sm_done"), sem("chain")
        tp_done, tp_out, agg_done, aggn_done, at_done, at_out, lhs_done, lhs_out = (
            sem(s) for s in ("tp_done", "tp_out", "agg_done", "aggn_done", "at_done", "at_out", "lhs_done", "lhs_out"))
        y_done, y_out = sem("y_done"), sem("y_out")
        block = ctx.enter_context(nc.Block())
        HP = 2 * UNITS
        LPH = 2 * UNITS
        LINKS = 10

        def rows(a, f, v):
            return a[bass.ds(f // 2, 1), :, bass.ds((f % 2) * REG + v * UROWS, UROWS), :].rearrange("a c r w -> (a c) (r w)")

        @block.sync
        def _(sp):
            with sp.Fori(0, halves) as f:
                for again in range(2):
                    def load(v, u):
                        sp.dma_start(xu[0:C, u, :], rows(x1, f, v)).then_inc(loaded[u], 16)

                    for u in range(2):
                        if again:
                            sp.wait_ge(prod_done, f * HP + 2 * (UNITS - 1 + u))
                        else:
                            sp.wait_ge(y_out, f * HP + 2)
                        load(u, u)
                    with sp.Fori(0, UNITS // 2 - 1) as j:
                        for u in range(2):
                            if again:
                                sp.wait_ge(y_out, f * HP + j * 4 + (2 * u + 4))
                            else:
                                sp.wait_ge(prod_done, f * HP + j * 4 + (2 * u + 2))
                            load(j * 2 + (u + 2), u)

        def wait_x(eng, f, again, j, u):
            eng.wait_ge(loaded[u], f * (16 * UNITS) + j * 16 + (again * 8 * UNITS + 16))

        @block.tensor
        def _(pe):
            pe.wait_ge(filled, 1)
            with pe.Fori(0, halves) as f:
                def products(s):
                    with pe.Fori(0, UPS // 2) as j:
                        for u in range(2):
                            wait_x(pe, f, 0, j + s * (UPS // 2), u)
                            for half in range(2):
                                n = f * HP + j * 4 + (s * 2 * UPS + 2 * u + half)
                                pe.wait_ge(out_done, n + 1)
                                for g in range(4):
                                    tile = 4 * half + g
                                    m = pe.matmul(psum[:, 2 * half + g // 2, 256 * (g % 2):256 * (g % 2) + NFC],
                                                  xu[:, u, 128 * tile:128 * tile + 128],
                                                  t["rhs"][:, bass.ds(f * 2 + tile % 2, 1), :].rearrange("p a n -> p (a n)"), start=True, stop=True)
                                m.then_inc(prod_done, 1)

                def aggregate(s):
                    b = s % 2
                    pe.wait_ge(sm_done, f * SU + (s + 1))
                    if s == 0:
                        pe.wait_ge(y_out, f * HP + 2)
                        pe.matmul(psum[0:EM, 4, 0:2 * VC], zero[:, 0:EM], zero[:], start=True, stop=False, skip_group_check=True)
                    for v in range(UPS):
                        bank = 5 + v % 2
                        n = f * UNITS + (s * UPS + v)
                        pe.wait_ge(tp_out, n + 1)
                        pe.matmul(psum[:, bank, 0:128], sm[:, b, NT * v:NT * v + NT, :].rearrange("p t e -> p (t e)"), t["eye"][:],
                                  start=True, stop=True).then_inc(tp_done, 1)
                        for g in range(NT):
                            tile = NT * v + g
                            m = pe.matmul(psum[0:EM, 4, VC * (g % 2):VC * (g % 2) + VC], sm[:, b, tile, :], val[:, b, tile, :],
                                          start=False, stop=(s == SU - 1 and tile >= TPS - 2), skip_group_check=True)
                    m.then_inc(agg_done, 1)

                for s in range(SU):
                    products(s)
                    if s:
                        aggregate(s - 1)
                aggregate(SU - 1)
                pe.wait_ge(tp_out, f * UNITS + (UNITS + 2))
                pe.wait_ge(aggn_done, f + 1)
                for i in range(2):
                    m = pe.matmul(psum[0:C, 5, i * EM:(i + 1) * EM], agg[:, i, :], t["eye"][0:EM, 0:EM], start=True, stop=True)
                m.then_inc(at_done, 1)
                pe.wait_ge(at_out, f + 1)
                for g in range(NT):
                    m = pe.matmul(psum[:, 6 + g // 4, C * (g % 4):C * (g % 4) + C], aggt[:, g, :], t["proj"][:], start=True, stop=True)
                m.then_inc(lhs_done, 1)
                with pe.Fori(0, UNITS) as v:
                    pe.wait_ge(lhs_out, f + 1)
                    for half in range(2):
                        n = f * HP + v * 2 + half
                        pe.wait_ge(y_out, n + 1)
                        for g in range(4):
                            m = pe.matmul(psum[0:C, 6 + half, 128 * g:128 * g + 128], lhs[:, 4 * half + g, :],
                                          smt[:, bass.ds(v, 1), :].rearrange("p a n -> p (a n)"), start=True, stop=True)
                        m.then_inc(y_done, 1)

        @block.scalar
        def _(act):
            act.sem_inc(out_done, 2)
            with act.Fori(0, halves) as f:
                for s in range(SU):
                    b = s % 2
                    with act.Fori(0, UPS) as j:
                        for half in range(2):
                            n = f * HP + j * 2 + (s * 2 * UPS + half)
                            act.wait_ge(prod_done, n + 1)
                            act.wait_ge(n2_done, n + 1)
                            pr = psum[:, 2 * half:2 * half + 2, :].rearrange("p a (b n) -> p (a b) n", b=2)
                            act.activation(sqf[:, half], pr[:, :, 0:C], ACT.Square).then_inc(sq_done, 1)
                            tiles = bass.ds(j * NT + 4 * half, 4)
                            act.activation(val[:, b, tiles, 0:C], pr[:, :, C:2 * C], ACT.Copy)
                            act.activation(dots[:, b, tiles, :], pr[:, :, 2 * C:NFC], ACT.Copy).then_inc(out_done, 1)
                    act.wait_ge(n2_done, f * HP + ((s + 1) * 2 * UPS + 2))
                    act.activation(nr[:], n2[:, b, :], ACT.Sqrt).then_inc(rt_done, 1)
                    act.wait_ge(sim_done, f * SU + (s + 1))
                    act.activation(sim[:], sim[:], ACT.Sigmoid, bias=t["beta"][:]).then_inc(sg_done, 1)

        @block.vector
        def _(dve):
            dve.sem_inc(n2_done, 2)
            dve.sem_inc(tp_out, 2)
            dve.sem_inc(y_out, 2)
            dve.memset(zero[:], 0.0)
            dve.memset(aggt[:], 0.0)
            dve.memset(val[:, :, :, C:VC], 1.0)
            dve.memset(xu[C:C + 1, :, :], 1.0).then_inc(filled, 1)
            with dve.Fori(0, halves) as f:
                def norms(s):
                    b = s % 2
                    with dve.Fori(0, UPS) as j:
                        for half in range(2):
                            n = f * HP + j * 2 + (s * 2 * UPS + half)
                            dve.wait_ge(sq_done, n + 1)
                            dve.tensor_reduce(n2[:, b, bass.ds(j * (NT * CH_HEADS) + half * 4 * CH_HEADS, 4 * CH_HEADS)],
                                              sqf[:, half].rearrange("p t (e c) -> p (t e) c", c=CH_DIM), AX.X, ALU.add).then_inc(n2_done, 1)

                def transposed(s):
                    for v in range(UPS):
                        dve.wait_ge(tp_done, f * UNITS + (s * UPS + v + 1))
                        dve.tensor_copy(smt[:, s * UPS + v, :], psum[:, 5 + v % 2, 0:128]).then_inc(tp_out, 1)

                def choose(s):
                    b = s % 2
                    done = [f * (SU * LINKS) + s * LINKS, 0]

                    def link(ins):
                        done[1] += 1
                        ins.then_inc(chain, 1)
                        dve.wait_ge(chain, done[0] + done[1])

                    dve.wait_ge(rt_done, f * SU + (s + 1))
                    link(dve.tensor_scalar(nr[:], nr[:], 1e-12, None, ALU.max))
                    link(dve.reciprocal(rn[:], nr[:]))
                    dve.wait_ge(out_done, f * HP + ((s + 1) * 2 * UPS + 2))
                    dve.tensor_tensor(sim[:], dots[:, b].rearrange("p t (e m) -> p (t e) m", m=NCTR),
                                      rn[:].unsqueeze(2).to_broadcast([128, NQ, NCTR]), ALU.mult).then_inc(sim_done, 1)
                    dve.wait_ge(sg_done, f * SU + (s + 1))
                    link(dve.tensor_reduce(top[:], sim[:], AX.X, ALU.max))
                    link(dve.tensor_tensor(hit[:], sim[:], top[:].unsqueeze(2).to_broadcast([128, NQ, NCTR]), ALU.is_equal))
                    link(dve.tensor_tensor(hit[:, :, 1], hit[:, :, 1], hit[:, :, 0], ALU.is_gt))
                    link(dve.tensor_tensor(got[:], hit[:, :, 1], hit[:, :, 0], ALU.max))
                    link(dve.tensor_tensor(hit[:, :, 2], hit[:, :, 2], got[:], ALU.is_gt))
                    link(dve.tensor_tensor(got[:], hit[:, :, 2], got[:], ALU.max))
                    link(dve.tensor_tensor(hit[:, :, 3], hit[:, :, 3], got[:], ALU.is_gt))
                    link(dve.tensor_tensor(sm[:, b].rearrange("p t (e m) -> p (t e) m", m=NCTR), sim[:], hit[:], ALU.mult))
                    dve.sem_inc(sm_done, 1)
                    assert done[1] == LINKS

                for s in range(SU):
                    norms(s)
                    if s:
                        transposed(s - 1)
                    choose(s)
                transposed(SU - 1)
                dve.wait_ge(agg_done, f * SU + SU)
                sums = psum[0:EM, 4, 0:2 * VC].rearrange("p (i n) -> p i n", n=VC)
                dve.tensor_scalar(den[:], sums[:, :, C], 1.0, None, ALU.add).then_inc(aggs, 1)
                dve.tensor_tensor(agg[:], sums[:, :, 0:C], t["value_centres"][:, bass.ds(f * 2, 2), :], ALU.add).then_inc(aggs, 1)
                dve.wait_ge(aggs, f * 4 + 2)
                dve.reciprocal(den[:], den[:]).then_inc(aggs, 1)
                dve.wait_ge(aggs, f * 4 + 3)
                dve.tensor_tensor(agg[:], agg[:], den[:].unsqueeze(2).to_broadcast([EM, 2, C]), ALU.mult).then_inc(aggs, 1)
                dve.wait_ge(aggs, f * 4 + 4)
                dve.tensor_tensor(agg[:], agg[:], t["own_channels"][:].unsqueeze(1).to_broadcast([EM, 2, C]), ALU.mult).then_inc(aggn_done, 1)
                dve.wait_ge(at_done, f + 1)
                for g in range(NT):
                    i = dve.tensor_copy(aggt[:, g, EM * g:EM * g + EM], psum[0:C, 5, (g % 2) * EM:(g % 2 + 1) * EM])
                i.then_inc(at_out, 1)
                dve.wait_ge(lhs_done, f + 1)
                for i in range(2):
                    ins = dve.tensor_copy(lhs[:, 4 * i:4 * i + 4, :], psum[:, 6 + i, 0:4 * C].rearrange("p (g n) -> p g n", n=C))
                ins.then_inc(lhs_out, 1)
                with dve.Fori(0, UNITS // 2) as j:
                    for u in range(2):
                        wait_x(dve, f, 1, j, u)
                        dve.wait_ge(stored[u], f * (8 * UNITS) + j * 16)
                        for half in range(2):
                            dve.wait_ge(y_done, f * HP + j * 4 + (2 * u + half + 1))
                            at = slice(512 * half, 512 * half + 512)
                            dve.scalar_tensor_tensor(out=ou[:, u, at], in0=psum[0:C, 6 + half, :], scalar=t["proj_b"][:, 0:1],
                                                           in1=xu[0:C, u, at], op0=ALU.add, op1=ALU.add).then_inc(y_out, 1)

        @block.gpsimd
        def _(pool):
            with pool.Fori(0, halves) as f:
                with pool.Fori(0, UNITS // 2) as j:
                    for u in range(2):
                        pool.wait_ge(y_out, f * HP + j * 4 + (2 * u + 4))
                        pool.dma_start(rows(out, f, j * 2 + u), ou[:, u, :]).then_inc(stored[u], 16)
            for u in range(2):
                pool.wait_ge(stored[u], 8 * UNITS * halves)


_NAMES = {"norm1_w": "L0_conv_norm1_w", "norm1_b": "L0_conv_norm1_b", "wq": "L0_conv_wq", "wk": "L0_conv_wk", "wv": "L0_conv_wv",
          "wproj": "L0_conv_wproj", "norm2_w": "L0_conv_norm2_w", "norm2_b": "L0_conv_norm2_b", "fc1_w": "L0_conv_fc1_w",
          "fc1_b": "L0_conv_fc1_b", "dw_w": "L0_conv_dw_w", "dw_b": "L0_conv_dw_b", "fc2_w": "L0_conv_fc2_w", "fc2_b": "L0_conv_fc2_b",
          "f_w": "L1_conv_f_w", "f_b": "L1_conv_f_b", "v_b": "L1_conv_v_b", "proj_b": "L1_conv_proj_b",
          "sim_alpha": "L1_conv_sim_alpha", "sim_beta": "L1_conv_sim_beta"}
_TRANSPOSED = {"f_wt": "L1_conv_f_w", "v_wt": "L1_conv_v_w", "proj_wt": "L1_conv_proj_w"}


def program(nc, p, out):
    x = p["x"]
    yln = nc.dram_tensor("y_attention", (B, C, H, W), F32).ap()
    x2 = nc.dram_tensor("x2", (B, C, H, W), F32).ap()
    x1 = nc.dram_tensor("x1", (B, C, H, W), F32).ap()
    ydr = nc.dram_tensor("y_mlp", (MLP, H, B, W), F32).ap()
    sdr = nc.dram_tensor("s_mlp", (NBLK, MLP, BLK, B, W), F32).ap()
    with ExitStack() as ctx:
        t = attention_tables(nc, ctx)
        group_norm_statistics(nc, x, t)
        attention_setup(nc, p, t)
        layer_norm(nc, x, yln, t)
        attention(nc, x, yln, x2, t)
    fc1(nc, p, x2, ydr)
    conv(nc, p, ydr, sdr)
    with ExitStack() as ctx:
        tab = {"row_sums": ctx.enter_context(nc.sbuf_tensor("row_sums", [C, B * H, 4], F32)),
               "squares": ctx.enter_context(nc.sbuf_tensor("squares", [C, B, 2 * NBLK + 2], F32))}
        t = cluster_tables(nc, ctx)
        fc2(nc, p, x, x2, sdr, x1, tab, True)
        fc2(nc, p, x, x2, sdr, x1, tab, False)
        cluster_setup(nc, p, tab, t)
        cluster(nc, x1, out, t)


def kernel(**inputs):
    import numpy as _np
    import concourse.bacc as _bacc
    from concourse import mybir as _mybir
    from concourse.bass_utils import run_bass_kernel_spmd as _run

    nc = _bacc.Bacc("TRN2", target_bir_lowering=False, num_devices=1)
    arrays = {"x": inputs["x"]}
    arrays.update({name: inputs[of] for name, of in _NAMES.items()})
    arrays.update({name: _np.asarray(inputs[of]).T for name, of in _TRANSPOSED.items()})
    arrays.update(constants())
    arrays.update(conv_constants())
    arrays.update(cluster_constants())
    p, feeds = {}, {}
    for name, a in arrays.items():
        a = _np.ascontiguousarray(a)
        feeds[f"in_{name}"] = a
        p[name] = nc.dram_tensor(f"in_{name}", a.shape, _mybir.dt.from_np(a.dtype), kind="ExternalInput").ap()
    out = nc.dram_tensor("out", (B, C, H, W), F32, kind="ExternalOutput").ap()
    program(nc, p, out)
    r = _run(nc, [feeds], core_ids=[0])
    return r.results[0]["out"]
```
